# Optimizing a Trainium2 kernel written in Bass

```python
import numpy as np
import jax
import jax.numpy as jnp

def _softmax(x, axis=-1):
    return jax.nn.softmax(x, axis=axis)

def _gelu(x):
    return jax.nn.gelu(x, approximate=True)

def _silu(x):
    return jax.nn.silu(x)

def _sigmoid(x):
    return jax.nn.sigmoid(x)

def _layernorm(x, axis=-1, eps=1e-05):
    m = jnp.mean(x, axis=axis, keepdims=True)
    v = jnp.var(x, axis=axis, keepdims=True)
    return (x - m) / jnp.sqrt(v + eps)

def _scatter_add(tgt, idx, src, axis=0):
    return tgt.at[idx].add(src)

def _segment_sum(src, seg, n):
    return jax.ops.segment_sum(src, seg, n)
kernel_name = 'mk_decoder_postln_d1_seqx_r8_3322b9'

def setup_inputs(seed: int=0):
    np.random.seed(seed)
    _w = jnp.asarray

    def _rec_inputs():
        import jax
        import jax.numpy as jnp
        _rk = jax.random.key(seed)
        x = 7.22e-05 + 1 * jax.random.normal(jax.random.fold_in(_rk, 1), (8, 256, 128), jnp.float32)
        _lenS = 256 - jax.random.randint(jax.random.fold_in(_rk, 7), (8,), 0, max(1, 256 // 4) + 1, jnp.int32)
        _lenS2 = 256 - jax.random.randint(jax.random.fold_in(_rk, 8), (8,), 0, max(1, 256 // 4) + 1, jnp.int32)
        _ctx_1024P = jax.random.normal(jax.random.fold_in(_rk, 11), (8, 16, 128), jnp.float32)
        _ctx_1024c = jax.random.dirichlet(jax.random.fold_in(_rk, 511), 0.3 * jnp.ones((16,), jnp.float32), (8, 256))
        _ctx_1024t = jnp.einsum('bsk,bkd->bsd', _ctx_1024c, _ctx_1024P)
        _ctx_1024t = _ctx_1024t * jax.lax.rsqrt(jnp.mean(jnp.square(_ctx_1024t)) + 1e-12) * 0.953939
        ctx_1024 = 4.13588e-05 + 0.999923 * (_ctx_1024t + 0.3 * jax.random.normal(jax.random.fold_in(_rk, 611), (8, 256, 128), jnp.float32))
        return (x, ctx_1024)
    x, ctx_1024 = _rec_inputs()

    def _L0_attn_setup():
        import jax, jax.numpy as jnp
        import numpy as np
        B, T, D = (4, 512, 128)
        H = 16
        DK = D // H
        EPS = 1e-06

        def _phi(x):
            return jax.nn.elu(x) + 1.0
        key = jax.random.key(seed)
        ks = jax.random.split(key, 9)
        s = 1.0 / np.sqrt(D)
        return {'x': jax.random.normal(ks[0], (B, T, D), dtype=jnp.float32), 'Wq': jax.random.uniform(ks[1], (D, D), jnp.float32, -s, s), 'bq': jax.random.uniform(ks[2], (D,), jnp.float32, -s, s), 'Wk': jax.random.uniform(ks[3], (D, D), jnp.float32, -s, s), 'bk': jax.random.uniform(ks[4], (D,), jnp.float32, -s, s), 'Wv': jax.random.uniform(ks[5], (D, D), jnp.float32, -s, s), 'bv': jax.random.uniform(ks[6], (D,), jnp.float32, -s, s), 'Wo': jax.random.uniform(ks[7], (D, D), jnp.float32, -s, s), 'bo': jax.random.uniform(ks[8], (D,), jnp.float32, -s, s)}
    _L0_attn_all = _L0_attn_setup()
    _L0_attn_in = {k: v for k, v in _L0_attn_all.items() if k in ('Wq', 'bq', 'Wk', 'bk', 'Wv', 'bv', 'Wo', 'bo')}
    del _L0_attn_all

    def _L0_xattn_setup():
        import jax, jax.numpy as jnp
        import numpy as np
        D_MODEL = 128
        HEADS = 16
        D_HEAD = D_MODEL // HEADS
        SEQ = 256
        C = 2
        K_TOP = int(C * np.log(SEQ))
        key = jax.random.key(seed)
        ks = jax.random.split(key, 5)
        s = 0.02
        return {'Q': jax.random.normal(ks[0], (4, SEQ, D_MODEL), jnp.float32), 'K': jax.random.normal(ks[1], (4, SEQ, D_MODEL), jnp.float32), 'V': jax.random.normal(ks[2], (4, SEQ, D_MODEL), jnp.float32), 'Wq': jax.random.normal(ks[3], (D_MODEL, D_HEAD), jnp.float32) * s, 'bq': jnp.zeros((D_HEAD,), jnp.float32), 'Wout': jax.random.normal(ks[4], (HEADS * D_HEAD, D_MODEL), jnp.float32) * s, 'bout': jnp.zeros((D_MODEL,), jnp.float32)}
    _L0_xattn_all = _L0_xattn_setup()
    _L0_xattn_in = {k: v for k, v in _L0_xattn_all.items() if k in ('Wq', 'bq', 'Wout', 'bout')}
    del _L0_xattn_all

    def _L0_ffn_setup():
        import jax, jax.numpy as jnp
        import numpy as np
        B, C, D = (2, 256, 128)
        I = 256
        E, K = (8, 2)
        CF = 1.25
        key = jax.random.key(seed)
        k1, k2, k3, k4 = jax.random.split(key, 4)
        scale = 0.02
        return {'hidden_states': jax.random.normal(k1, (B, C, D), jnp.float32), 'Wg': jax.random.normal(k2, (E, D), jnp.float32) * scale, 'W1': jax.random.normal(k3, (E, D, 2 * I), jnp.float32) * scale, 'W2': jax.random.normal(k4, (E, I, D), jnp.float32) * scale}
    _L0_ffn_all = _L0_ffn_setup()
    _L0_ffn_in = {k: v for k, v in _L0_ffn_all.items() if k in ('Wg', 'W1', 'W2')}
    del _L0_ffn_all
    return {'x': x, 'ctx_1024': ctx_1024, 'L0_attn_Wq': _L0_attn_in['Wq'], 'L0_attn_bq': _L0_attn_in['bq'], 'L0_attn_Wk': _L0_attn_in['Wk'], 'L0_attn_bk': _L0_attn_in['bk'], 'L0_attn_Wv': _L0_attn_in['Wv'], 'L0_attn_bv': _L0_attn_in['bv'], 'L0_attn_Wo': _L0_attn_in['Wo'], 'L0_attn_bo': _L0_attn_in['bo'], 'L0_xattn_Wq': _L0_xattn_in['Wq'], 'L0_xattn_bq': _L0_xattn_in['bq'], 'L0_xattn_Wout': _L0_xattn_in['Wout'], 'L0_xattn_bout': _L0_xattn_in['bout'], 'L0_ffn_Wg': _L0_ffn_in['Wg'], 'L0_ffn_W1': _L0_ffn_in['W1'], 'L0_ffn_W2': _L0_ffn_in['W2']}

def reference(x, ctx_1024, L0_attn_Wq, L0_attn_bq, L0_attn_Wk, L0_attn_bk, L0_attn_Wv, L0_attn_bv, L0_attn_Wo, L0_attn_bo, L0_xattn_Wq, L0_xattn_bq, L0_xattn_Wout, L0_xattn_bout, L0_ffn_Wg, L0_ffn_W1, L0_ffn_W2):
    import jax
    import jax.numpy as jnp

    def _L0_attn_ref(x, Wq, bq, Wk, bk, Wv, bv, Wo, bo):
        import jax, jax.numpy as jnp
        import numpy as np
        B, T, D = (4, 512, 128)
        H = 16
        DK = D // H
        EPS = 1e-06

        def _phi(x):
            return jax.nn.elu(x) + 1.0
        Bq, Tq, _ = x.shape

        def heads(y):
            return y.reshape(Bq, Tq, H, DK).transpose(0, 2, 1, 3)
        q = _phi(heads(x @ Wq.T + bq))
        k = _phi(heads(x @ Wk.T + bk))
        v = heads(x @ Wv.T + bv)
        kv = jnp.einsum('bhtd,bhtm->bhdm', k, v)
        z = 1.0 / (jnp.einsum('bhtd,bhd->bht', q, k.sum(axis=2) + EPS) + EPS)
        out = jnp.einsum('bhtd,bhdm,bht->bhtm', q, kv, z)
        out = out.transpose(0, 2, 1, 3).reshape(Bq, Tq, -1)
        return out @ Wo.T + bo

    def _L0_xattn_ref(Q, K, V, Wq, bq, Wout, bout):
        import jax, jax.numpy as jnp
        import numpy as np
        D_MODEL = 128
        HEADS = 16
        D_HEAD = D_MODEL // HEADS
        SEQ = 256
        C = 2
        K_TOP = int(C * np.log(SEQ))
        B, L, _ = Q.shape
        q = (Q @ Wq + bq).transpose(0, 2, 1)
        k_ = (K @ Wq + bq).transpose(0, 2, 1)
        v = (V @ Wq + bq).transpose(0, 2, 1)
        Qf = jnp.fft.fft(q.astype(jnp.complex64))
        Kf = jnp.fft.fft(k_.astype(jnp.complex64))
        corr = jnp.real(jnp.fft.ifft(Qf * jnp.conj(Kf)))
        corr = corr.mean(axis=(0, 1))
        W_topk, I_topk = jax.lax.top_k(corr, K_TOP)
        W_topk = jax.nn.softmax(W_topk)

        def body(R, ws):
            w, shift = ws
            return (R + w * jnp.roll(v, -shift, axis=-1), None)
        R3, _ = jax.lax.scan(body, jnp.zeros_like(v), (W_topk, I_topk))
        R = jnp.broadcast_to(R3[:, None], (B, HEADS, D_HEAD, L)).reshape(B, L, HEADS * D_HEAD)
        return R @ Wout + bout

    def _L0_ffn_ref(hidden_states, Wg, W1, W2):
        import jax, jax.numpy as jnp
        import numpy as np
        B, C, D = (2, 256, 128)
        I = 256
        E, K = (8, 2)
        CF = 1.25
        Bx, Cx, d = hidden_states.shape
        N = Bx * Cx
        cap = int(N * K * CF / E)
        x = hidden_states.reshape(N, d)
        logits = x @ Wg.T
        top_v, top_i = jax.lax.top_k(logits, K)
        gates = jax.nn.softmax(top_v, axis=-1)
        flat_e = top_i.reshape(N * K)
        gates_f = gates.reshape(N * K)
        tok = jnp.repeat(jnp.arange(N), K)
        onehot = jax.nn.one_hot(flat_e, E, dtype=jnp.int32)
        pos = jnp.cumsum(onehot, axis=0) - 1
        pos_f = jnp.take_along_axis(pos, flat_e[:, None], axis=1)[:, 0]
        keep = pos_f < cap
        pos_safe = jnp.where(keep, pos_f, cap)
        exp_batches = jnp.zeros((E, cap, d), x.dtype).at[flat_e, pos_safe].set(x[tok], mode='drop')
        h = jnp.einsum('ecd,edf->ecf', exp_batches, W1)
        inp, gate = jnp.split(h, 2, axis=-1)
        h = jax.nn.gelu(inp, approximate=False) * gate
        exp_out = jnp.einsum('eci,eid->ecd', h, W2)
        gathered = exp_out[flat_e, jnp.minimum(pos_safe, cap - 1)]
        contrib = jnp.where(keep, gates_f, 0.0)[:, None] * gathered
        out = jax.ops.segment_sum(contrib, tok, num_segments=N)
        return out.reshape(Bx, Cx, d)
    x = _layernorm(x + _L0_attn_ref(x, L0_attn_Wq, L0_attn_bq, L0_attn_Wk, L0_attn_bk, L0_attn_Wv, L0_attn_bv, L0_attn_Wo, L0_attn_bo), axis=-1)
    x = _layernorm(x + _L0_xattn_ref(x, ctx_1024, ctx_1024, L0_xattn_Wq, L0_xattn_bq, L0_xattn_Wout, L0_xattn_bout), axis=-1)
    x = _layernorm(x + _L0_ffn_ref(x, L0_ffn_Wg, L0_ffn_W1, L0_ffn_W2), axis=-1)
    return x

_drawn_inputs = setup_inputs


def setup_inputs(seed=0):
    import zlib

    import numpy as np

    out = dict(_drawn_inputs(seed))
    spreads = {'L0_xattn_bq': (0.0, 0.1), 'L0_xattn_bout': (0.0, 0.1)}
    factors = {'L0_attn_Wq': 8.0,
     'L0_attn_bq': 8.0,
     'L0_attn_Wk': 8.0,
     'L0_attn_bk': 8.0,
     'L0_attn_Wv': 2.823,
     'L0_ffn_Wg': 8.0,
     'L0_ffn_W1': 8.0,
     'L0_ffn_W2': 8.0}
    for name, (base, spread) in spreads.items():
        noise = np.random.default_rng([zlib.crc32(name.encode()), seed]).standard_normal(out[name].shape)
        drawn = base * np.exp(spread * noise) if base else spread * noise
        out[name] = jnp.asarray(drawn.astype(out[name].dtype))
    for name, factor in factors.items():
        out[name] = (out[name] * factor).astype(out[name].dtype)
    return out
```

```python
from contextlib import ExitStack

import concourse.bass as bass
from concourse import mybir

F32 = mybir.dt.float32
F16 = mybir.dt.float16
I32 = mybir.dt.int32
U32 = mybir.dt.uint32
ALU = mybir.AluOpType
ACT = mybir.ActivationFunctionType
AX = mybir.AxisListType

P = 128
B, S, D = 8, 256, 128
N = B * S
NT = N // P
HEADS, DK = 16, 8
XC = 8
TOPK = 11
E, K2 = 8, 2
FF = 256
CAP = N * K2 * 5 // 4 // E
NBLK = CAP // P
DENSE = 2
SPARSE = E - DENSE
LN_EPS = 1e-5
ATT_EPS = 1e-6
ROW = D + E
LOW = -3.0e38
RSQRT_SEED = float(0x5F3759DF)

W_Q, W_KV, W_BQ, W_O, W_XQ, W_XO, W_G, W_END = 0, 128, 384, 385, 513, 521, 649, 657
V_KV, V_O, V_XQ, V_XO, V_END = 0, 256, 384, 392, 520
T_ID, T_HEAD, T_SCALE, T_TIE, T_SLOT, T_BLK, T_LANE, T_TOK, T_TRI, T_END = (
    0, 128, 272, 280, 288, 296, 336, 464, 480, 608)


class Order:

    def __init__(self, eng, sem):
        self.eng, self.sem, self.n = eng, sem, 0

    def done(self, ins):
        self.n += 1
        ins.then_inc(self.sem, 1)
        self.eng.wait_ge(self.sem, self.n)


def units():
    dense = [(e, 4 * g, 4) for g in range(NT // 4) for e in range(DENSE)]
    sparse = [(e, b0, n) for e in range(DENSE, E) for b0, n in ((0, 3), (3, 2))]
    return dense, sparse


def decoder_layer(nc, xt, xr, ctxt, weights, vectors, tables, dft, idft, w1, w2, out):
    ctx = ExitStack()
    with ctx:
        def sb(name, shape, dt=F32):
            return ctx.enter_context(nc.sbuf_tensor(name, shape, dt))

        def sem(name):
            return ctx.enter_context(nc.semaphore(name))

        rows_d = nc.dram_tensor("rows_d", [N, ROW], F32, kind="Internal").ap()
        acc_d = nc.dram_tensor("acc_d", [N, D], F32, kind="Internal").ap()

        xT = sb("xT", [P, N])
        x = sb("x", [P, NT, D])
        ctxT = sb("ctxT", [P, N])
        W = sb("W", [P, W_END])
        vec = sb("vec", [P, V_END])
        tab = sb("tab", [P, T_END])
        fwd = sb("fwd", [P, 2, S])
        inv = sb("inv", [P, 2, S])
        W1 = sb("W1", [P, E, 2 * FF])
        W2 = sb("W2", [P, E, 2, D])
        ident = tab[:, T_ID:T_ID + P]
        tri16 = sb("tri16", [P, P], F16)
        ones16 = sb("ones16", [P, P], F16)
        lane16 = sb("lane16", [P, P], F16)

        kv = sb("kv", [P, 2, 2, 2 * D + 1])
        kneg = sb("kneg", [P, 2, D])
        kexp = sb("kexp", [P, 2, D])
        kphi = sb("kphi", [P, 2, 2, D])
        qrel = sb("qrel", [P, S])
        qexp = sb("qexp", [P, S])
        qphi = sb("qphi", [P, 2, S])
        ksum = sb("ksum", [P, 1])
        kvm = sb("kvm", [P, 2, D + HEADS])
        z0 = sb("z0", [P, 2, HEADS])
        z1 = sb("z1", [P, 2, HEADS])
        o = sb("o", [P, 2, D])
        oT = sb("oT", [P, 2, S])
        r = sb("r", [P, NT, D])
        stats = sb("stats", [P, NT, 6])
        mv = sb("mv", [P, NT, 2])
        var = sb("var", [P, NT])
        half = sb("half", [P, NT], I32)
        rs = sb("rs", [P, NT])
        ra = sb("ra", [P, NT])
        x1 = sb("x1", [P, NT, D])
        x1T = sb("x1T", [P, 2, S])
        kc = sb("kc", [P, 2, B * XC])
        qc = sb("qc", [P, 2, B * XC])
        kf = sb("kf", [P, 2, B * XC])
        k1 = sb("k1", [P, 2, B * XC])
        k2 = sb("k2", [P, 2, B * XC])
        va = sb("va", [P, 2, B * XC])
        vb = sb("vb", [P, 2, B * XC])
        junk = sb("junk", [P, S])
        s1 = sb("s1", [P, 1])
        s2 = sb("s2", [P, 1])
        top1 = sb("top1", [P, 8])
        top2 = sb("top2", [P, 8])
        ntop = sb("ntop", [P, 1])
        corr1 = sb("corr1", [P, S])
        corr2 = sb("corr2", [P, S])
        cexp = sb("cexp", [P, S])
        cw = sb("cw", [P, S])
        csum = sb("csum", [P, 1])
        crec = sb("crec", [P, 1])
        wa = sb("wa", [P, 1])
        wb = sb("wb", [P, 1])
        xf = sb("xf", [P, 2, B * XC])
        rT = sb("rT", [P, B, 16])
        rTw = sb("rTw", [P, B, P // 16, 16])
        x2g = sb("x2g", [P, NT, ROW])
        x2T = sb("x2T", [P, N])
        lg = sb("lg", [P, NT, E])
        ma = sb("ma", [P, 2, NT])
        eq = sb("eq", [P, NT, E])
        km = sb("km", [P, NT])
        oh = sb("oh", [P, 2, NT, E])
        m16 = sb("m16", [P, NT, E], F16)
        gd = sb("gd", [P, NT])
        ge = sb("ge", [P, NT])
        gs = sb("gs", [P, NT])
        g1 = sb("g1", [P, NT])
        g2 = sb("g2", [P, NT])
        ga = sb("ga", [P, NT, E])
        gb = sb("gb", [P, NT, E])
        sv = sb("sv", [P, NT, E])
        ohs = sb("ohs", [P, 2, NT, E])
        slot_f = sb("slot_f", [P, 2 * NT])
        slot = sb("slot", [P, 2 * NT], I32)
        sblk = sb("sblk", [P, 2 * NT], I32)
        slane_i = sb("slane_i", [P, 2 * NT], I32)
        slane = sb("slane", [P, 2 * NT])
        NI = SPARSE * NBLK
        ohb = sb("ohb", [P, 2 * NT, NI], F16)
        ohl = sb("ohl", [P, 2 * NT, P], F16)
        idf = sb("idf", [P, NI])
        idx = sb("idx", [P, NI], U32)
        xe = sb("xe", [P, SPARSE, NBLK, ROW])
        xeT = sb("xeT", [P, 2, 3 * P])
        NH = 5
        gel = sb("gel", [P, 2, 4 * P])
        hT = sb("hT", [P, NH, 2, 4 * P])
        ye = sb("ye", [P, SPARSE, NBLK, D])
        dacc = r
        acc = ctxT[:, :].rearrange("p (t d) -> p t d", d=D)
        res = xT[:, :].rearrange("p (t d) -> p t d", d=D)
        zero = sb("zero", [P, 4 * D])

        bank = [ctx.enter_context(nc.psum_tensor(f"bank{i}", [P, 512], F32)) for i in range(8)]
        pq = bank[0][:, 0:S]
        pkv = bank[1][:, :].rearrange("p (t n) -> p t n", t=2)
        pkk = bank[2][:, 0:D + 1]
        pnum = bank[3][:, :].rearrange("p (t n) -> p t n", t=2)
        poT = bank[4][:, 0:S]
        py = bank[5][:, 0:S].rearrange("p (t n) -> p t n", t=2)
        px1T = bank[6][:, 0:S]
        pc = bank[7][:, 0:P].rearrange("p (t b c) -> p t b c", t=2, b=B)
        pkf = bank[7][:, P:2 * P].rearrange("p (a n) -> p a n", a=2)
        pqf = bank[2][:, 0:P].rearrange("p (a n) -> p a n", a=2)
        pcorr = bank[3][:, 0:S]
        prT = bank[4][:, 0:P].rearrange("p (h n) -> p h n", h=2)
        pO = [bank[6][:, :].rearrange("p (b n) -> p b n", b=4), bank[7][:, :].rearrange("p (b n) -> p b n", b=4)]
        plg = bank[2][:, 0:P].rearrange("p (t e) -> p t e", e=E)
        ppos = bank[2][:, P:2 * P].rearrange("p (t e) -> p t e", e=E)
        pidx = bank[2][:, 2 * P:2 * P + NI]
        pT = bank[5]
        pH = [bank[0], bank[1], bank[3], bank[4]]
        pY = [bank[6][:, :].rearrange("p (t n) -> p t n", n=D), bank[7][:, :].rearrange("p (t n) -> p t n", n=D)]

        ld_w = sem("ld_w")
        ld_w2 = sem("ld_w2")
        ld_vec = sem("ld_vec")
        ld_tab = sem("ld_tab")
        ld_xT = [sem(f"ld_xT{i}") for i in range(4)]
        ld_x = sem("ld_x")
        ld_ctx = sem("ld_ctx")
        ld_dft = sem("ld_dft")
        ld_moe = sem("ld_moe")
        zero_set = sem("zero_set")
        acc_zeroed = sem("acc_zeroed")
        consts_set = sem("consts_set")
        xe_set = sem("xe_set")
        ones_set = sem("ones_set")
        xbias = sem("xbias")
        dve_o = sem("dve_o")
        act_o = sem("act_o")
        pool_o = sem("pool_o")
        kv_raw = sem("kv_raw")
        kv_biased = sem("kv_biased")
        k_low = sem("k_low")
        k_exp = sem("k_exp")
        k_phi = sem("k_phi")
        q_raw = sem("q_raw")
        q_parts = sem("q_parts")
        q_phi = sem("q_phi")
        kk_raw = sem("kk_raw")
        kk_masked = sem("kk_masked")
        num_raw = sem("num_raw")
        o_ready = sem("o_ready")
        oT_raw = sem("oT_raw")
        oT_copied = sem("oT_copied")
        y_raw = sem("y_raw")
        y_summed = sem("y_summed")
        x1_ready = sem("x1_ready")
        x1_biased = sem("x1_biased")
        x1T_raw = sem("x1T_raw")
        x1T_copied = sem("x1T_copied")
        kc_raw = sem("kc_raw")
        kc_ready = sem("kc_ready")
        kf_raw = sem("kf_raw")
        kf_ready = sem("kf_ready")
        qc_raw = sem("qc_raw")
        qc_ready = sem("qc_ready")
        qf_raw = sem("qf_raw")
        spec_ready = sem("spec_ready")
        corr_raw = sem("corr_raw")
        top_ready = sem("top_ready")
        c_exp = sem("c_exp")
        xf_ready = sem("xf_ready")
        rT_raw = sem("rT_raw")
        rT_copied = sem("rT_copied")
        O_raw = sem("O_raw")
        x2_ready = sem("x2_ready")
        x2T_raw = sem("x2T_raw")
        x2T_copied = sem("x2T_copied")
        lg_raw = sem("lg_raw")
        pair_ready = sem("pair_ready")
        pos_raw = sem("pos_raw")
        diff_ready = sem("diff_ready")
        gate_exp = sem("gate_exp")
        gates_ready = sem("gates_ready")
        onehots = sem("onehots")
        idx_raw = sem("idx_raw")
        idx_ready = sem("idx_ready")
        rows_out = sem("rows_out")
        gathered = [sem(f"gathered{e}") for e in range(SPARSE)]
        added = sem("added")
        xeT_raw = sem("xeT_raw")
        xeT_copied = sem("xeT_copied")
        h_raw = sem("h_raw")
        h_gelu = sem("h_gelu")
        h_ready = sem("h_ready")
        ye_raw = sem("ye_raw")
        ye_taken = sem("ye_taken")
        ld_acc = sem("ld_acc")
        out_ready = sem("out_ready")
        out_stored = sem("out_stored")

        dense, sparse = units()
        every = dense + sparse
        DLAG = 3

        def sparse_unit(u):
            return u - len(dense)

        block = ctx.enter_context(nc.Block())

        @block.sync
        def _(sp):
            sp.dma_start(W[:, 0:W_O], weights[:, 0:W_O]).then_inc(ld_w, 16)
            sp.dma_start(xT[:, 0:512], xt[:, 0:512]).then_inc(ld_xT[0], 16)
            sp.dma_start(vec[:, :], vectors.partition_broadcast(P)).then_inc(ld_vec, 16)
            sp.dma_start(tab[:, :], tables).then_inc(ld_tab, 16)
            sp.dma_start(x[:, :, :], xr.rearrange("(t p) d -> p t d", p=P)).then_inc(ld_x, 16)
            for i in range(1, 4):
                sp.dma_start(xT[:, 512 * i:512 * (i + 1)], xt[:, 512 * i:512 * (i + 1)]).then_inc(ld_xT[i], 16)
            sp.dma_start(W[:, W_O:], weights[:, W_O:]).then_inc(ld_w2, 16)
            sp.dma_start(ctxT[:, :], ctxt).then_inc(ld_ctx, 16)
            sp.dma_start(fwd[:, :, :], dft).then_inc(ld_dft, 16)
            sp.dma_start(inv[:, :, :], idft).then_inc(ld_dft, 16)
            sp.dma_start(W1[:, :, :], w1.rearrange("e d f -> d e f")).then_inc(ld_moe, 16)
            sp.dma_start(W2[:, :, :, :], w2.rearrange("e (c f) d -> f e c d", f=P)).then_inc(ld_moe, 16)
            sp.wait_ge(zero_set, 1)
            for g in range(4):
                sp.dma_start(acc_d.rearrange("(g p t) d -> g p (t d)", g=4, p=P)[g], zero[:, :]).then_inc(acc_zeroed, 16)
            sp.wait_ge(gates_ready, 1)
            sp.dma_start(rows_d.rearrange("(t p) d -> p t d", p=P), x2g[:, :, :]).then_inc(rows_out, 16)
            sp.wait_ge(added, 16 * NBLK * SPARSE)
            for g in range(4):
                sp.dma_start(acc[:, 4 * g:4 * g + 4, :],
                             acc_d[512 * g:512 * (g + 1), :].rearrange("(t p) d -> p t d", p=P)).then_inc(ld_acc, 16)
                sp.wait_ge(ld_acc, 16 * (g + 1))
            for g in range(4):
                sp.wait_ge(out_ready, g + 1)
                sp.dma_start(out[512 * g:512 * (g + 1), :].rearrange("(t p) d -> p t d", p=P),
                             res[:, 4 * g:4 * g + 4, :]).then_inc(out_stored, 16)
            sp.wait_ge(out_stored, 64)

        @block.tensor
        def _(pe):
            def project_kv(b):
                pe.wait_ge(ld_xT[b // 2], 16)
                if b >= 1:
                    pe.wait_ge(kv_biased, b)
                for t in range(2):
                    j = 2 * b + t
                    last = nc.tensor.matmul(pkv[:, t, :], xT[:, P * j:P * (j + 1)], W[:, W_KV:W_KV + 2 * D],
                                            start=True, stop=True)
                last.then_inc(kv_raw, 1)

            def project_q(b):
                if b >= 1:
                    pe.wait_ge(q_parts, 2 * b)
                nc.tensor.matmul(pq, W[:, W_Q:W_Q + D], xT[:, S * b:S * (b + 1)], start=True, stop=True).then_inc(q_raw, 1)

            def keys_values(b):
                pe.wait_ge(k_phi, b + 1)
                pe.wait_ge(kv_biased, b + 1)
                if b == 0:
                    pe.wait_ge(ones_set, 1)
                if b >= 1:
                    pe.wait_ge(kk_masked, b)
                for t in range(2):
                    last = nc.tensor.matmul(pkk, kphi[:, b % 2, t, :], kv[:, b % 2, t, D:2 * D + 1],
                                            start=(t == 0), stop=(t == 1))
                last.then_inc(kk_raw, 1)

            def attend(b):
                pe.wait_ge(kk_masked, b + 1)
                pe.wait_ge(q_phi, b + 1)
                if b >= 1:
                    pe.wait_ge(o_ready, b)
                for t in range(2):
                    last = nc.tensor.matmul(pnum[:, t, 0:D + HEADS], qphi[:, b % 2, P * t:P * (t + 1)],
                                            kvm[:, b % 2, :], start=True, stop=True)
                last.then_inc(num_raw, 1)

            def turn_o(b):
                pe.wait_ge(o_ready, b + 1)
                if b == 0:
                    pe.wait_ge(ld_tab, 16)
                if b >= 1:
                    pe.wait_ge(oT_copied, b)
                for t in range(2):
                    last = nc.tensor.transpose(poT[:, P * t:P * (t + 1)], o[:, t, :], ident)
                last.then_inc(oT_raw, 1)

            def project_o(b):
                pe.wait_ge(oT_copied, b + 1)
                if b == 0:
                    pe.wait_ge(ld_w2, 16)
                if b >= 1:
                    pe.wait_ge(y_summed, b)
                for t in range(2):
                    last = nc.tensor.matmul(py[:, t, :], oT[:, b % 2, P * t:P * (t + 1)], W[:, W_O:W_O + D],
                                            start=True, stop=True)
                last.then_inc(y_raw, 1)

            def project_ctx(b):
                if b == 0:
                    pe.wait_ge(ld_ctx, 16)
                    pe.wait_ge(ld_w2, 16)
                for t in range(2):
                    j = 2 * b + t
                    last = nc.tensor.matmul(pc[:, t, b, :], ctxT[:, P * j:P * (j + 1)], W[:, W_XQ:W_XQ + XC],
                                            start=True, stop=True)
                last.then_inc(kc_raw, 1)

            def spectrum(into, of):
                for a in range(2):
                    for t in range(2):
                        last = nc.tensor.matmul(into[:, a, :], fwd[:, t, P * a:P * (a + 1)], of[:, t, :],
                                                start=(t == 0), stop=(t == 1))
                return last

            def turn_x1(b):
                pe.wait_ge(x1_ready, b // 2 + 1)
                if b >= 1:
                    pe.wait_ge(x1T_copied, b)
                for t in range(2):
                    last = nc.tensor.transpose(px1T[:, P * t:P * (t + 1)], x1[:, 2 * b + t, :], ident)
                last.then_inc(x1T_raw, 1)

            def project_x1(b):
                pe.wait_ge(x1T_copied, b + 1)
                if b == 0:
                    pe.wait_ge(kf_ready, 1)
                for t in range(2):
                    last = nc.tensor.matmul(pc[:, t, b, :], x1T[:, b % 2, P * t:P * (t + 1)], W[:, W_XQ:W_XQ + XC],
                                            start=True, stop=True)
                last.then_inc(qc_raw, 1)

            pe.wait_ge(ld_w, 16)
            for i in range(12):
                if i < B:
                    project_kv(i)
                if 1 <= i <= B:
                    keys_values(i - 1)
                if i < B:
                    project_q(i)
                if 1 <= i <= B:
                    attend(i - 1)
                if 2 <= i <= B + 1:
                    project_o(i - 2)
                if 1 <= i <= 4:
                    project_ctx(2 * i - 2)
                    project_ctx(2 * i - 1)
                if i == 6:
                    pe.wait_ge(kc_ready, 1)
                    pe.wait_ge(ld_dft, 32)
                    spectrum(pkf, kc).then_inc(kf_raw, 1)
                if 1 <= i <= B:
                    turn_o(i - 1)
                if i >= 8:
                    for b in range(B):
                        if max(8, 2 * (b // 2) + 4) == i:
                            turn_x1(b)
                            project_x1(b)

            pe.wait_ge(qc_ready, 1)
            spectrum(pqf, qc).then_inc(qf_raw, 1)
            pe.wait_ge(spec_ready, 1)
            nc.tensor.matmul(pcorr, s1[:, 0:1].broadcast_to([P, P]), inv[:, 0, :], start=True, stop=False)
            nc.tensor.matmul(pcorr, s2[:, 0:1].broadcast_to([P, P]), inv[:, 1, :], start=False, stop=True).then_inc(corr_raw, 1)
            pe.wait_ge(xf_ready, 1)
            for h in range(2):
                for a in range(2):
                    last = nc.tensor.matmul(prT[:, h, :], inv[:, a, P * h:P * (h + 1)], xf[:, a, :],
                                            start=(a == 0), stop=(a == 1))
            last.then_inc(rT_raw, 1)
            for b in range(B):
                if b % 4 == 0:
                    pe.wait_ge(rT_copied, b // 4 + 1)
                last = nc.tensor.matmul(pO[b // 4][:, b % 4, :], rTw[:, b, :, :].rearrange("p n k -> p (n k)"),
                                        W[:, W_XO:W_XO + D], start=True, stop=True)
                if b % 4 == 3:
                    last.then_inc(O_raw, 1)

            def turn_x2(g):
                pe.wait_ge(x2_ready, g + 1)
                if g >= 1:
                    pe.wait_ge(x2T_copied, g)
                for t in range(4):
                    last = nc.tensor.transpose(pT[:, P * t:P * (t + 1)], x2g[:, 4 * g + t, 0:D], ident)
                last.then_inc(x2T_raw, 1)

            def logits(g):
                pe.wait_ge(x2T_copied, g + 1)
                for t in range(4):
                    j = 4 * g + t
                    last = nc.tensor.matmul(plg[:, j, :], x2T[:, P * j:P * (j + 1)], W[:, W_G:W_G + E],
                                            start=True, stop=True)
                last.then_inc(lg_raw, 1)

            def up(u):
                e, t0, n = every[u]
                if u == 0:
                    pe.wait_ge(ld_moe, 32)
                rhs = x2T[:, P * t0:P * (t0 + n)] if u < len(dense) else xeT[:, u % 2, 0:P * n]
                for f, h in enumerate((0, 2, 1, 3)):
                    if u >= 1:
                        pe.wait_ge(h_gelu if h < 2 else h_ready, 2 * u - 1 + h % 2)
                    nc.tensor.matmul(pH[h][:, 0:P * n], W1[:, e, P * h:P * (h + 1)], rhs,
                                     start=True, stop=True).then_inc(h_raw, 1)

            def down(u):
                e, t0, n = every[u]
                pe.wait_ge(h_ready, 2 * (u + 1))
                if u == 0:
                    pe.wait_ge(x2_ready, 4)
                if u >= 2:
                    pe.wait_ge(ye_taken, u - 1)
                for t in range(n):
                    for c in range(2):
                        last = nc.tensor.matmul(pY[u % 2][:, t, :], hT[:, u % NH, c, P * t:P * (t + 1)], W2[:, e, c, :],
                                                start=(c == 0), stop=(c == 1))
                last.then_inc(ye_raw, 1)

            def turn_xe(u):
                s = sparse_unit(u)
                e, b0, n = every[u]
                pe.wait_ge(gathered[e - DENSE], 16 * NBLK)
                if s >= 1:
                    pe.wait_ge(xeT_copied, s)
                for t in range(n):
                    last = nc.tensor.transpose(pT[:, P * t:P * (t + 1)], xe[:, e - DENSE, b0 + t, 0:D], ident)
                last.then_inc(xeT_raw, 1)

            for g in range(4):
                turn_x2(g)
                logits(g)
            for u in range(len(dense)):
                if u == 2:
                    pe.wait_ge(pair_ready, 1)
                    nc.tensor.matmul(ppos, tri16[:, :], m16[:, :, :], start=True, stop=False, skip_group_check=True)
                    for i in range(NT - 1):
                        last = nc.tensor.matmul(ppos[:, i + 1:, :], ones16[:, :],
                                                m16[:, i:i + 1, :].broadcast_to([P, NT - 1 - i, E]),
                                                start=False, stop=(i == NT - 2), skip_group_check=True)
                    last.then_inc(pos_raw, 1)
                if u == 5:
                    pe.wait_ge(onehots, 1)
                    for i in range(2 * NT):
                        last = nc.tensor.matmul(pidx, ohl[:, i, :], ohb[:, i, :], start=(i == 0), stop=(i == 2 * NT - 1))
                    last.then_inc(idx_raw, 1)
                up(u)
                if u >= DLAG:
                    down(u - DLAG)
            for u in range(len(dense) - DLAG, len(dense)):
                down(u)
            n = len(dense)
            turn_xe(n)
            for u in range(n, len(every)):
                pe.wait_ge(xeT_copied, sparse_unit(u) + 1)
                up(u)
                if u + 1 < len(every):
                    turn_xe(u + 1)
                if u > n:
                    down(u - 1)
            down(len(every) - 1)

        @block.scalar
        def _(act):
            def q_half(b):
                act.wait_ge(q_raw, b + 1)
                if b >= 1:
                    act.wait_ge(q_phi, b)
                nc.scalar.activation(qexp[:, :], pq, ACT.Exp, bias=W[:, W_BQ:W_BQ + 1]).then_inc(q_parts, 1)
                nc.scalar.activation(qrel[:, :], pq, ACT.Relu, bias=W[:, W_BQ:W_BQ + 1]).then_inc(q_parts, 1)

            def k_half(b):
                act.wait_ge(k_low, b + 1)
                if b >= 1:
                    act.wait_ge(k_phi, b)
                nc.scalar.activation(kexp[:, :, :], kneg[:, :, :], ACT.Exp).then_inc(k_exp, 1)

            def copy_oT(b):
                act.wait_ge(oT_raw, b + 1)
                if b >= 2:
                    act.wait_ge(y_raw, b - 1)
                nc.scalar.activation(oT[:, b % 2, :], poT, ACT.Copy).then_inc(oT_copied, 1)

            def copy_x1T(b):
                act.wait_ge(x1T_raw, b + 1)
                if b >= 2:
                    act.wait_ge(qc_raw, b - 1)
                nc.scalar.activation(x1T[:, b % 2, :], px1T, ACT.Copy).then_inc(x1T_copied, 1)

            act.wait_ge(ld_w, 16)
            for i in range(12):
                if i < B:
                    q_half(i)
                    k_half(i)
                if 1 <= i <= B:
                    copy_oT(i - 1)
                if i >= 8:
                    for b in range(B):
                        if max(8, 2 * (b // 2) + 4) == i:
                            copy_x1T(b)
            act.wait_ge(top_ready, 1)
            nc.scalar.activation(cexp[:, :], pcorr, ACT.Exp, bias=ntop[:, 0:1]).then_inc(c_exp, 1)
            for g in range(4):
                act.wait_ge(x2T_raw, g + 1)
                nc.scalar.activation(x2T[:, 512 * g:512 * (g + 1)], pT[:, :], ACT.Copy).then_inc(x2T_copied, 1)
            act.wait_ge(diff_ready, 1)
            nc.scalar.activation(ge[:, :], gd[:, :], ACT.Exp).then_inc(gate_exp, 1)

            def gelu(u):
                e, t0, n = every[u]
                for c in range(2):
                    act.wait_ge(h_raw, 4 * u + (1 if c == 0 else 3))
                    if u >= 1:
                        act.wait_ge(h_ready, 2 * u - 1 + c)
                    nc.scalar.activation(gel[:, c, 0:P * n], pH[c][:, 0:P * n], ACT.Gelu).then_inc(h_gelu, 1)

            def copy_xe(u):
                s = sparse_unit(u)
                e, b0, n = every[u]
                act.wait_ge(xeT_raw, s + 1)
                if s >= 2:
                    act.wait_ge(h_raw, 4 * (u - 1))
                nc.scalar.activation(xeT[:, u % 2, 0:P * n], pT[:, 0:P * n], ACT.Copy).then_inc(xeT_copied, 1)

            for u in range(len(dense)):
                gelu(u)
            n = len(dense)
            copy_xe(n)
            for u in range(n, len(every)):
                gelu(u)
                if u + 1 < len(every):
                    copy_xe(u + 1)

        @block.gpsimd
        def _(pool):
            order = Order(pool, pool_o)
            nc.gpsimd.memset(kv[:, :, :, 2 * D:2 * D + 1], 1.0).then_inc(ones_set, 1)
            nc.gpsimd.memset(zero[:, :], 0.0).then_inc(zero_set, 1)
            nc.gpsimd.memset(ones16[:, :], 1.0).then_inc(consts_set, 1)
            nc.gpsimd.memset(xe[:, :, :, :], 0.0).then_inc(xe_set, 1)

            def phi_k(b):
                pool.wait_ge(kv_biased, b + 1)
                if b >= 1:
                    pool.wait_ge(k_exp, b)
                if b >= 2:
                    pool.wait_ge(kk_raw, b - 1)
                k = kv[:, b % 2, :, 0:D]
                nc.gpsimd.tensor_scalar(kneg[:, :, :], k, 0.0, None, ALU.min).then_inc(k_low, 1)
                order.done(nc.gpsimd.tensor_scalar(kphi[:, b % 2, :, :], k, 0.0, None, ALU.max))
                pool.wait_ge(k_exp, b + 1)
                nc.gpsimd.tensor_tensor(kphi[:, b % 2, :, :], kphi[:, b % 2, :, :], kexp[:, :, :], ALU.add).then_inc(k_phi, 1)

            def bias_x(b):
                j = 2 * b
                nc.gpsimd.tensor_tensor(x[:, j:j + 2, :], x[:, j:j + 2, :],
                                        vec[:, V_O:V_O + D].unsqueeze(1).broadcast_to([P, 2, D]), ALU.add).then_inc(xbias, 1)

            def bias_x1(b):
                pool.wait_ge(x1T_raw, b + 1)
                j = 2 * b
                nc.gpsimd.tensor_tensor(x1[:, j:j + 2, :], x1[:, j:j + 2, :],
                                        vec[:, V_XO:V_XO + D].unsqueeze(1).broadcast_to([P, 2, D]), ALU.add).then_inc(x1_biased, 1)

            for i in range(12):
                if i < B:
                    phi_k(i)
                    if i == 0:
                        pool.wait_ge(ld_x, 16)
                        pool.wait_ge(ld_vec, 16)
                    bias_x(i)
                if i >= 8:
                    for b in range(B):
                        if max(8, 2 * (b // 2) + 4) == i:
                            bias_x1(b)

            def gather(s):
                for b in range(NBLK):
                    i = s * NBLK + b
                    nc.gpsimd.indirect_dma_start(
                        xe[:, s, b, :], None, rows_d[:, :],
                        bass.IndirectOffsetOnAxis(ap=idx[:, i:i + 1], axis=0),
                        bounds_check=N - 1, oob_is_err=False).then_inc(gathered[s], 16)

            def add_rows(s):
                pool.wait_ge(ye_taken, len(dense) + 2 * (s + 1))
                if s >= 1:
                    pool.wait_ge(added, 16 * NBLK * s)
                for b in range(NBLK):
                    i = s * NBLK + b
                    nc.gpsimd.indirect_dma_start(
                        acc_d[:, :], bass.IndirectOffsetOnAxis(ap=idx[:, i:i + 1], axis=0),
                        ye[:, s, b, :], None, bounds_check=N - 1, oob_is_err=COMPUTE_OOB,
                        compute_op=ALU.add).then_inc(added, 16)

            pool.wait_ge(xe_set, 1)
            pool.wait_ge(idx_ready, 1)
            pool.wait_ge(rows_out, 16)
            pool.wait_ge(acc_zeroed, 64)
            gather(0)
            gather(1)
            for s in range(SPARSE):
                if s + 2 < SPARSE:
                    gather(s + 2)
                add_rows(s)

        @block.vector
        def _(dve):
            order = Order(dve, dve_o)
            tt, ts, stt = nc.vector.tensor_tensor, nc.vector.tensor_scalar, nc.vector.scalar_tensor_tensor

            def bias_kv(b):
                dve.wait_ge(kv_raw, b + 1)
                if b >= 2:
                    dve.wait_ge(kk_raw, b - 1)
                tt(kv[:, b % 2, :, 0:2 * D], pkv, vec[:, V_KV:V_KV + 2 * D].unsqueeze(1).broadcast_to([P, 2, 2 * D]),
                   ALU.add).then_inc(kv_biased, 1)

            def phi_q(b):
                dve.wait_ge(q_parts, 2 * (b + 1))
                if b >= 2:
                    dve.wait_ge(num_raw, b - 1)
                stt(qphi[:, b % 2, :], qexp[:, :], 1.0, qrel[:, :], ALU.min, ALU.add).then_inc(q_phi, 1)

            def mask_kk(b):
                dve.wait_ge(kk_raw, b + 1)
                if b == 0:
                    dve.wait_ge(ld_tab, 16)
                if b >= 2:
                    dve.wait_ge(num_raw, b - 1)
                order.done(ts(ksum[:, :], pkk[:, D:D + 1], ATT_EPS, None, ALU.add))
                tt(kvm[:, b % 2, 0:D], pkk[:, 0:D], tab[:, T_HEAD:T_HEAD + D], ALU.mult)
                ts(kvm[:, b % 2, D:], tab[:, T_HEAD + D:T_HEAD + D + HEADS], ksum[:, 0:1], None, ALU.mult).then_inc(kk_masked, 1)

            def normalise(b):
                dve.wait_ge(num_raw, b + 1)
                if b >= 1:
                    dve.wait_ge(oT_raw, b)
                order.done(ts(z0[:, :, :], pnum[:, :, D:D + HEADS], ATT_EPS, None, ALU.add))
                order.done(nc.vector.reciprocal(z1[:, :, :], z0[:, :, :]))
                tt(o[:, :, :].rearrange("p t (h c) -> p t h c", c=DK),
                   pnum[:, :, 0:D].rearrange("p t (h c) -> p t h c", c=DK),
                   z1[:, :, :].unsqueeze(3).broadcast_to([P, 2, HEADS, DK]), ALU.mult).then_inc(o_ready, 1)

            def residual1(b):
                dve.wait_ge(y_raw, b + 1)
                dve.wait_ge(xbias, b + 1)
                j = 2 * b
                ins = tt(r[:, j:j + 2, :], py, x[:, j:j + 2, :], ALU.add)
                ins.then_inc(y_summed, 1)
                dve.wait_ge(y_summed, b + 1)
                for t in range(j, j + 2):
                    last = nc.vector.bn_stats(stats[:, t, :], r[:, t, :])
                order.done(last)
                for t in range(j, j + 2):
                    last = nc.vector.bn_aggr(mv[:, t, :], stats[:, t, :])
                order.done(last)

            def rsqrt(t0, t1):
                v, h, y, a = var[:, t0:t1], half[:, t0:t1], rs[:, t0:t1], ra[:, t0:t1]
                order.done(ts(v, mv[:, t0:t1, 1:2].rearrange("p t o -> p (t o)"), LN_EPS, None, ALU.add))
                order.done(ts(h, v.bitcast(I32), 1, None, ALU.logical_shift_right))
                order.done(ts(y.bitcast(I32), h, -1.0, RSQRT_SEED, ALU.mult, ALU.add))
                for _ in range(3):
                    order.done(stt(a, y, -0.5, y, ALU.mult, ALU.mult))
                    order.done(tt(a, a, v, ALU.mult))
                    order.done(stt(y, a, 1.5, y, ALU.add, ALU.mult))

            def apply_norm(to, t0, t1):
                for t in range(t0, t1):
                    last = ts(to(t), r[:, t, :], mv[:, t, 0:1], rs[:, t:t + 1], ALU.subtract, ALU.mult)
                return last

            def prepare_k():
                dve.wait_ge(kf_raw, 1)
                order.done(nc.vector.tensor_copy(kf[:, :, :], pkf))
                c = [tab[:, T_SCALE + i:T_SCALE + i + 1] for i in range(8)]
                ka, kb = kf[:, 0, :], kf[:, 1, :]
                ts(k1[:, 0, :], ka, c[0], None, ALU.mult)
                ts(k1[:, 1, :], kb, c[1], None, ALU.mult)
                ts(k2[:, 0, :], kb, c[2], None, ALU.mult)
                ts(k2[:, 1, :], ka, c[1], None, ALU.mult)
                ts(va[:, 0, :], ka, c[4], None, ALU.mult)
                ts(va[:, 1, :], kb, c[5], None, ALU.mult)
                ts(vb[:, 0, :], kb, c[5], None, ALU.mult)
                order.done(ts(vb[:, 1, :], ka, c[6], None, ALU.mult))
                stt(k2[:, 1, :], kb, c[3], k2[:, 1, :], ALU.mult, ALU.add)
                ins = stt(vb[:, 1, :], kb, c[7], vb[:, 1, :], ALU.mult, ALU.add)
                ins.then_inc(kf_ready, 1)

            dve.wait_ge(ld_vec, 16)
            for i in range(10):
                if i < B:
                    bias_kv(i)
                if 1 <= i <= B:
                    mask_kk(i - 1)
                if i < B:
                    phi_q(i)
                if 1 <= i <= B:
                    normalise(i - 1)
                if i == 1:
                    nc.vector.tensor_copy(lane16[:, :], tab[:, T_LANE:T_LANE + P])
                    nc.vector.tensor_copy(tri16[:, :], tab[:, T_TRI:T_TRI + P]).then_inc(consts_set, 1)
                if 2 <= i <= B + 1:
                    residual1(i - 2)
                    if i % 2:
                        t0 = 2 * (i - 3)
                        rsqrt(t0, t0 + 4)
                        apply_norm(lambda t: x1[:, t, :], t0, t0 + 4).then_inc(x1_ready, 1)
                if i == 5:
                    dve.wait_ge(kc_raw, B)
                    tt(kc[:, :, :].rearrange("p t (b c) -> p t b c", c=XC), pc,
                       vec[:, V_XQ:V_XQ + XC].unsqueeze(1).unsqueeze(1).broadcast_to([P, 2, B, XC]), ALU.add).then_inc(kc_ready, 1)
                if i == 7:
                    prepare_k()

            dve.wait_ge(qc_raw, B)
            tt(qc[:, :, :].rearrange("p t (b c) -> p t b c", c=XC), pc,
               vec[:, V_XQ:V_XQ + XC].unsqueeze(1).unsqueeze(1).broadcast_to([P, 2, B, XC]), ALU.add).then_inc(qc_ready, 1)
            dve.wait_ge(qf_raw, 1)
            dve.wait_ge(kf_ready, 1)
            qf = pqf.rearrange("p a n -> p (a n)")
            order.done(nc.vector.tensor_tensor_reduce(
                out=junk[:, 0:P], in0=qf, in1=k1[:, :, :].rearrange("p a n -> p (a n)"), scale=1.0, scalar=0.0,
                op0=ALU.mult, op1=ALU.add, accum_out=s1[:, :]))
            nc.vector.tensor_tensor_reduce(
                out=junk[:, 0:P], in0=qf, in1=k2[:, :, :].rearrange("p a n -> p (a n)"), scale=1.0, scalar=0.0,
                op0=ALU.mult, op1=ALU.add, accum_out=s2[:, :]).then_inc(spec_ready, 1)
            dve.wait_ge(corr_raw, 1)
            order.done(nc.vector.max(top1[:, :], pcorr))
            order.done(nc.vector.match_replace(corr1[:, :], top1[:, :], pcorr, LOW))
            ts(ntop[:, :], top1[:, 0:1], -1.0, None, ALU.mult).then_inc(top_ready, 1)
            order.done(nc.vector.max(top2[:, :], corr1[:, :]))
            order.done(nc.vector.memset(top2[:, TOPK - 8:], LOW))
            order.done(nc.vector.match_replace(corr2[:, :], top2[:, :], corr1[:, :], LOW))
            dve.wait_ge(c_exp, 1)
            order.done(stt(cw[:, :], corr2[:, :], LOW, cexp[:, :], ALU.is_equal, ALU.mult, accum_out=csum[:, :]))
            order.done(nc.vector.reciprocal(crec[:, :], csum[:, :]))
            for a, w in ((0, wa), (1, wb)):
                order.done(nc.vector.tensor_tensor_reduce(
                    out=junk[:, :], in0=cw[:, :], in1=inv[:, a, :], scale=crec[:, 0:1], scalar=0.0,
                    op0=ALU.mult, op1=ALU.add, accum_out=w[:, :]))
            order.done(ts(xf[:, :, :], va[:, :, :], wa[:, 0:1], None, ALU.mult))
            stt(xf[:, :, :], vb[:, :, :], wb[:, 0:1], xf[:, :, :], ALU.mult, ALU.add).then_inc(xf_ready, 1)
            dve.wait_ge(rT_raw, 1)
            order.done(nc.vector.tensor_copy(rT[:, :, :].rearrange("p b (c h) -> p h b c", h=2),
                                             prT.rearrange("p h (b c) -> p h b c", c=XC)))
            for b in (0, 4):
                nc.vector.tensor_copy(rTw[:, b:b + 4, :, :],
                                      rT[:, b:b + 4, :].unsqueeze(2).broadcast_to([P, 4, P // 16, 16])).then_inc(rT_copied, 1)
            for g in range(4):
                for b in (2 * g, 2 * g + 1):
                    if b % 4 == 0:
                        dve.wait_ge(O_raw, b // 4 + 1)
                    dve.wait_ge(x1_biased, b + 1)
                    j = 2 * b
                    last = tt(r[:, j:j + 2, :], x1[:, j:j + 2, :],
                              pO[b // 4][:, b % 4:b % 4 + 1, :].broadcast_to([P, 2, D]), ALU.add)
                order.done(last)
                for t in range(4 * g, 4 * g + 4):
                    last = nc.vector.bn_stats(stats[:, t, :], r[:, t, :])
                order.done(last)
                for t in range(4 * g, 4 * g + 4):
                    last = nc.vector.bn_aggr(mv[:, t, :], stats[:, t, :])
                order.done(last)
                rsqrt(4 * g, 4 * g + 4)
                apply_norm(lambda t: x2g[:, t, 0:D], 4 * g, 4 * g + 4).then_inc(x2_ready, 1)

            def gating(u):
                e, t0, n = every[u]
                for c in range(2):
                    dve.wait_ge(h_gelu, 2 * u + 1 + c)
                    dve.wait_ge(h_raw, 4 * u + (2 if c == 0 else 4))
                    if u >= NH:
                        dve.wait_ge(ye_raw, u - NH + 1)
                    tt(hT[:, u % NH, c, 0:P * n], pH[2 + c][:, 0:P * n], gel[:, c, 0:P * n], ALU.mult).then_inc(h_ready, 1)

            def over_e(a):
                return a.unsqueeze(2).broadcast_to([P, NT, E])

            def pick(k, src):
                order.done(nc.vector.tensor_reduce(ma[:, k, :], src, AX.X, ALU.max))
                order.done(tt(eq[:, :, :], src, over_e(ma[:, k, :]), ALU.is_equal))
                order.done(tt(eq[:, :, :], eq[:, :, :],
                              tab[:, T_TIE:T_TIE + E].unsqueeze(1).broadcast_to([P, NT, E]), ALU.mult))
                order.done(nc.vector.tensor_reduce(km[:, :], eq[:, :, :], AX.X, ALU.max))
                order.done(tt(oh[:, k, :, :], eq[:, :, :], over_e(km[:, :]), ALU.is_equal))

            def route_experts():
                dve.wait_ge(lg_raw, 4)
                order.done(nc.vector.tensor_copy(lg[:, :, :], plg))
                pick(0, lg[:, :, :])
                order.done(stt(lg[:, :, :], oh[:, 0, :, :], LOW, lg[:, :, :], ALU.mult, ALU.add))
                pick(1, lg[:, :, :])
                tt(m16[:, :, :], oh[:, 0, :, :], oh[:, 1, :, :], ALU.add).then_inc(pair_ready, 1)
                tt(gd[:, :], ma[:, 1, :], ma[:, 0, :], ALU.subtract).then_inc(diff_ready, 1)

            def route_gates():
                dve.wait_ge(gate_exp, 1)
                order.done(ts(gs[:, :], ge[:, :], 1.0, None, ALU.add))
                order.done(nc.vector.reciprocal(g1[:, :], gs[:, :]))
                order.done(tt(g2[:, :], ge[:, :], g1[:, :], ALU.mult))
                tt(ga[:, :, :], oh[:, 0, :, :], over_e(g1[:, :]), ALU.mult)
                order.done(tt(gb[:, :, :], oh[:, 1, :, :], over_e(g2[:, :]), ALU.mult))
                order.done(tt(ga[:, :, :], ga[:, :, :], gb[:, :, :], ALU.add))
                dve.wait_ge(pos_raw, 1)
                stt(x2g[:, :, D:], ppos, float(CAP), ga[:, :, :], ALU.is_lt, ALU.mult).then_inc(gates_ready, 1)

            def route_slots():
                order.done(tt(sv[:, :, :], ppos, tab[:, T_SLOT:T_SLOT + E].unsqueeze(1).broadcast_to([P, NT, E]), ALU.add))
                order.done(ts(eq[:, :, :], ppos, float(CAP), float(E * CAP * 2), ALU.is_ge, ALU.mult))
                order.done(tt(sv[:, :, :], sv[:, :, :], eq[:, :, :], ALU.add))
                for k in range(2):
                    last = tt(ohs[:, k, :, :], oh[:, k, :, :], sv[:, :, :], ALU.mult)
                order.done(last)
                order.done(nc.vector.tensor_reduce(slot_f[:, :], ohs[:, :, :, :].rearrange("p k t e -> p (k t) e"), AX.X, ALU.add))
                order.done(nc.vector.tensor_copy(slot[:, :], slot_f[:, :]))
                ts(sblk[:, :], slot[:, :], 7, None, ALU.logical_shift_right)
                order.done(ts(slane_i[:, :], slot[:, :], P - 1, None, ALU.bitwise_and))
                order.done(nc.vector.tensor_copy(slane[:, :], slane_i[:, :]))

            def route_onehots(i0, i1):
                for i in range(i0, i1):
                    j = i % NT
                    last = ts(ohl[:, i, :], lane16[:, :], slane[:, i:i + 1], tab[:, T_TOK + j:T_TOK + j + 1],
                              ALU.is_equal, ALU.mult)
                if i1 == 2 * NT:
                    tt(ohb[:, :, :], tab[:, T_BLK + DENSE * NBLK:T_BLK + E * NBLK].unsqueeze(1).broadcast_to([P, 2 * NT, NI]),
                       sblk[:, :].unsqueeze(2).broadcast_to([P, 2 * NT, NI]), ALU.is_equal).then_inc(onehots, 1)

            def route_index():
                dve.wait_ge(idx_raw, 1)
                order.done(ts(idf[:, :], pidx, 0.0, float(4 * N), ALU.is_equal, ALU.mult))
                order.done(tt(idf[:, :], idf[:, :], pidx, ALU.add))
                ts(idx[:, :], idf[:, :], -1.0, None, ALU.add).then_inc(idx_ready, 1)

            def take_dense(u):
                e, t0, n = every[u]
                dve.wait_ge(ye_raw, u + 1)
                dve.wait_ge(gates_ready, 1)
                if u >= 1:
                    dve.wait_ge(ye_taken, u)
                for t in range(n):
                    j = t0 + t
                    base = x2g[:, j, 0:D] if e == 0 else dacc[:, j, :]
                    last = stt(dacc[:, j, :], pY[u % 2][:, t, :], x2g[:, j, D + e:D + e + 1], base, ALU.mult, ALU.add)
                last.then_inc(ye_taken, 1)

            def take_sparse(u):
                e, b0, n = every[u]
                s = e - DENSE
                dve.wait_ge(ye_raw, u + 1)
                tt(ye[:, s, b0:b0 + n, :], pY[u % 2][:, 0:n, :],
                   xe[:, s, b0:b0 + n, D + e:D + e + 1].broadcast_to([P, n, D]), ALU.mult).then_inc(ye_taken, 1)

            route_experts()
            gating(0)
            gating(1)
            route_gates()
            gating(2)
            route_slots()
            gating(3)
            route_onehots(0, 16)
            take_dense(0)
            gating(4)
            route_onehots(16, 32)
            take_dense(1)
            for u in range(5, len(dense)):
                gating(u)
                if u == 5:
                    route_index()
                take_dense(u - DLAG)
            for u in range(len(dense) - DLAG, len(dense)):
                take_dense(u)
            n = len(dense)
            for u in range(n, len(every)):
                gating(u)
                if u > n:
                    take_sparse(u - 1)
            take_sparse(len(every) - 1)
            for g in range(4):
                t0, t1 = 4 * g, 4 * g + 4
                dve.wait_ge(ld_acc, 16 * (g + 1))
                order.done(tt(r[:, t0:t1, :], dacc[:, t0:t1, :], acc[:, t0:t1, :], ALU.add))
                for t in range(t0, t1):
                    last = nc.vector.bn_stats(stats[:, t, :], r[:, t, :])
                order.done(last)
                for t in range(t0, t1):
                    last = nc.vector.bn_aggr(mv[:, t, :], stats[:, t, :])
                order.done(last)
                rsqrt(t0, t1)
                apply_norm(lambda t: res[:, t, :], t0, t1).then_inc(out_ready, 1)


COMPUTE_OOB = False


def kernel(x, ctx_1024, L0_attn_Wq, L0_attn_bq, L0_attn_Wk, L0_attn_bk, L0_attn_Wv, L0_attn_bv, L0_attn_Wo,
           L0_attn_bo, L0_xattn_Wq, L0_xattn_bq, L0_xattn_Wout, L0_xattn_bout, L0_ffn_Wg, L0_ffn_W1, L0_ffn_W2):
    import numpy as np
    import concourse.bacc as bacc
    from concourse.bass_utils import run_bass_kernel_spmd

    a = np.asarray
    xr = np.ascontiguousarray(a(x).reshape(N, D))
    weights = np.concatenate([a(L0_attn_Wq).T, a(L0_attn_Wk).T, a(L0_attn_Wv).T, a(L0_attn_bq).reshape(D, 1),
                              a(L0_attn_Wo).T, a(L0_xattn_Wq), a(L0_xattn_Wout), a(L0_ffn_Wg).T], axis=1)
    vectors = np.concatenate([a(L0_attn_bk), a(L0_attn_bv), a(L0_attn_bo), a(L0_xattn_bq), a(L0_xattn_bout)])

    p = np.arange(P)[:, None]
    tab = np.zeros((P, T_END), np.float32)
    tab[:, T_ID:T_ID + P] = np.eye(P)
    tab[:, T_HEAD:T_HEAD + D] = p // DK == np.arange(D)[None] // DK
    tab[:, T_HEAD + D:T_HEAD + D + HEADS] = p // DK == np.arange(HEADS)[None]
    scale = np.where(p[:, 0] == 0, 1.0, 2.0) / S
    rest = np.where(p[:, 0] == 0, 0.0, 1.0)
    mean = 1.0 / (B * XC)
    for i, c in enumerate([scale * mean, scale * rest * mean, -scale * rest * mean, scale * (1 - rest) * mean,
                           scale, scale * rest, -scale * rest, scale * (1 - rest)]):
        tab[:, T_SCALE + i] = c
    tab[:, T_TIE:T_TIE + E] = E - np.arange(E)
    tab[:, T_SLOT:T_SLOT + E] = CAP * np.arange(E)
    tab[:, T_BLK:T_BLK + E * NBLK] = np.arange(E * NBLK)
    tab[:, T_LANE:T_LANE + P] = np.arange(P)
    tab[:, T_TOK:T_TOK + NT] = p + P * np.arange(NT)[None] + 1
    tab[:, T_TRI:T_TRI + P] = p < np.arange(P)[None]
    time, turn = np.arange(S)[:, None], np.arange(P)[None]
    angle = 2 * np.pi * ((time * turn) % S) / S
    basis = np.concatenate([np.cos(angle), np.sin(angle)], axis=1)
    basis[:, P] = 1 - 2 * (np.arange(S) % 2)
    dft = basis.reshape(2, P, S).transpose(1, 0, 2)
    idft = basis.T.reshape(2, P, S).transpose(1, 0, 2)

    arrays = {
        "xt": np.ascontiguousarray(xr.T), "xr": xr, "ctxt": np.ascontiguousarray(a(ctx_1024).reshape(N, D).T),
        "weights": np.ascontiguousarray(weights), "vectors": vectors, "tables": tab,
        "dft": np.ascontiguousarray(dft.astype(np.float32)), "idft": np.ascontiguousarray(idft.astype(np.float32)),
        "w1": np.ascontiguousarray(a(L0_ffn_W1)), "w2": np.ascontiguousarray(a(L0_ffn_W2)),
    }
    nc = bacc.Bacc("TRN2", target_bir_lowering=False, num_devices=1)
    args = [nc.dram_tensor(f"in_{name}", v.shape, mybir.dt.from_np(v.dtype), kind="ExternalInput").ap()
            for name, v in arrays.items()]
    out = nc.dram_tensor("out", (N, D), F32, kind="ExternalOutput").ap()
    decoder_layer(nc, *args, out)
    got = run_bass_kernel_spmd(nc, [{f"in_{name}": v for name, v in arrays.items()}], core_ids=[0])
    return got.results[0]["out"].reshape(B, S, D)
```

```python
from contextlib import ExitStack

import concourse.bass as bass
from concourse import mybir

F32 = mybir.dt.float32
F16 = mybir.dt.float16
I32 = mybir.dt.int32
U32 = mybir.dt.uint32
ALU = mybir.AluOpType
ACT = mybir.ActivationFunctionType
AX = mybir.AxisListType

P = 128
B, S, D = 8, 256, 128
N = B * S
NT = N // P
HEADS, DK = 16, 8
XC = 8
TOPK = 11
E, K2 = 8, 2
FF = 256
CAP = N * K2 * 5 // 4 // E
NBLK = CAP // P
DENSE = 2
SPARSE = E - DENSE
LN_EPS = 1e-5
ATT_EPS = 1e-6
ROW = D + E
LOW = -3.0e38

W_Q, W_K, W_BQ, W_BK, W_V, W_O, W_XQ, W_XO, W_G, W_END = 0, 128, 256, 257, 258, 386, 514, 522, 650, 658
V_V, V_O, V_XQ, V_XO, V_END = 0, 128, 256, 264, 392
T_ID, T_HEAD, T_SCALE, T_EXP, T_SLOT, T_BLK, T_LANE, T_TOK, T_TRI, T_END = (
    0, 128, 272, 280, 288, 296, 336, 464, 480, 608)
RSQRT_SEED = float(0x5F1FFFF9)
RSQRT_A, RSQRT_B = 0.703952253, 0.703952253 * 2.38924456
RSQRT_OPS = 9
ROUNDS = 14
ROUND_X1 = [10, 10, 11, 11, 12, 12, 13, 13]


class Order:

    def __init__(self, eng, sem):
        self.eng, self.sem, self.n = eng, sem, 0

    def mark(self, ins):
        self.n += 1
        ins.then_inc(self.sem, 1)
        return self.n

    def wait(self, n):
        self.eng.wait_ge(self.sem, n)

    def done(self, ins):
        self.n += 1
        ins.then_inc(self.sem, 1)
        self.eng.wait_ge(self.sem, self.n)


def units():
    dense = [(e, 4 * g, 4) for g in range(NT // 4) for e in range(DENSE)]
    sparse = [(e, b0, n) for e in range(DENSE, E) for b0, n in ((0, 3), (3, 2))]
    return dense, sparse


def decoder_layer(nc, xt, xr, ctxt, weights, vectors, tables, dft, idft, w1, w2, out):
    ctx = ExitStack()
    with ctx:
        def sb(name, shape, dt=F32):
            return ctx.enter_context(nc.sbuf_tensor(name, shape, dt))

        def sem(name):
            return ctx.enter_context(nc.semaphore(name))

        rows_d = nc.dram_tensor("rows_d", [N, ROW], F32, kind="Internal").ap()
        acc_d = nc.dram_tensor("acc_d", [N, D], F32, kind="Internal").ap()

        xT = sb("xT", [P, N])
        x = sb("x", [P, NT, D])
        ctxT = sb("ctxT", [P, N])
        W = sb("W", [P, W_END])
        vec = sb("vec", [P, V_END])
        tab = sb("tab", [P, T_END])
        fwd = sb("fwd", [P, 2, S])
        inv = sb("inv", [P, 2, S])
        W1 = sb("W1", [P, E, 2 * FF])
        W2 = sb("W2", [P, E, 2, D])
        ident = tab[:, T_ID:T_ID + P]
        tri16 = sb("tri16", [P, P], F16)
        ones16 = sb("ones16", [P, P], F16)
        lane16 = sb("lane16", [P, P], F16)

        v = sb("v", [P, 2, 2, D + HEADS])
        qke = sb("qke", [P, 2, 2, S])
        qkr = sb("qkr", [P, 2, 2, S])
        phi = sb("phi", [P, 2, 2, S])
        kphi = sb("kphi", [P, 2, 2, D])
        kvm = sb("kvm", [P, 2, D + HEADS])
        z0 = sb("z0", [P, 2, HEADS])
        z1 = sb("z1", [P, 2, HEADS])
        o = sb("o", [P, 2, 2, D])
        oT = sb("oT", [P, 2, S])
        r = sb("r", [P, NT, D])
        stats = sb("stats", [P, NT, 6])
        mv = sb("mv", [P, NT, 2])
        var = sb("var", [P, NT])
        half = sb("half", [P, NT], I32)
        rs = sb("rs", [P, NT])
        ra = sb("ra", [P, NT])
        nmr = sb("nmr", [P, NT])
        x1 = sb("x1", [P, NT, D])
        x1T = sb("x1T", [P, 2, S])
        kc = sb("kc", [P, 2, B * XC])
        qc = sb("qc", [P, 2, B * XC])
        kf = sb("kf", [P, 2, B * XC])
        k1 = sb("k1", [P, 2, B * XC])
        k2 = sb("k2", [P, 2, B * XC])
        va = sb("va", [P, 2, B * XC])
        vb = sb("vb", [P, 2, B * XC])
        junk = sb("junk", [P, S])
        s1 = sb("s1", [P, 1])
        s2 = sb("s2", [P, 1])
        top1 = sb("top1", [P, 8])
        top2 = sb("top2", [P, 8])
        ntop = sb("ntop", [P, 1])
        corr1 = sb("corr1", [P, S])
        corr2 = sb("corr2", [P, S])
        cexp = sb("cexp", [P, S])
        cw = sb("cw", [P, S])
        csum = sb("csum", [P, 1])
        crec = sb("crec", [P, 1])
        wa = sb("wa", [P, 1])
        wb = sb("wb", [P, 1])
        xf = sb("xf", [P, 2, B * XC])
        rT = sb("rT", [P, B, 16])
        rTw = sb("rTw", [P, B, P // 16, 16])
        x2g = sb("x2g", [P, NT, ROW])
        x2T = sb("x2T", [P, N])
        lg = sb("lg", [P, NT, E])
        top = sb("top", [P, NT, 8])
        topi = sb("topi", [P, NT, 8], U32)
        pick = sb("pick", [P, 2, NT])
        oh = sb("oh", [P, 2, NT, E])
        m16 = sb("m16", [P, NT, E], F16)
        gd = sb("gd", [P, NT])
        ge = sb("ge", [P, NT])
        gs = sb("gs", [P, NT])
        g1 = sb("g1", [P, NT])
        g2 = sb("g2", [P, NT])
        ga = sb("ga", [P, NT, E])
        gb = sb("gb", [P, NT, E])
        sv = sb("sv", [P, NT, E])
        over = sb("over", [P, NT, E])
        ohs = sb("ohs", [P, 2, NT, E])
        slot_f = sb("slot_f", [P, 2 * NT])
        slot = sb("slot", [P, 2 * NT], I32)
        sblk = sb("sblk", [P, 2 * NT], I32)
        slane_i = sb("slane_i", [P, 2 * NT], I32)
        slane = sb("slane", [P, 2 * NT])
        tokh = sb("tokh", [P, NT])
        NI = SPARSE * NBLK
        ohb = sb("ohb", [P, 2 * NT, NI], F16)
        ohl = sb("ohl", [P, 2 * NT, P], F16)
        idf = sb("idf", [P, NI])
        idx = sb("idx", [P, NI], U32)
        xe = sb("xe", [P, SPARSE, NBLK, ROW])
        xeT = sb("xeT", [P, 2, 3 * P])
        NH = 5
        gel = sb("gel", [P, 2, 4 * P])
        hT = sb("hT", [P, NH, 2, 4 * P])
        ye = sb("ye", [P, SPARSE, NBLK, D])
        dacc = r
        acc = ctxT[:, :].rearrange("p (t d) -> p t d", d=D)
        res = xT[:, :].rearrange("p (t d) -> p t d", d=D)
        zero = sb("zero", [P, 4 * D])

        bank = [ctx.enter_context(nc.psum_tensor(f"bank{i}", [P, 512], F32)) for i in range(8)]
        pqk = bank[0][:, :].rearrange("p (a n) -> p a n", a=2)
        pv = bank[1][:, 0:S].rearrange("p (t n) -> p t n", t=2)
        pkT = bank[2][:, 0:S].rearrange("p (t n) -> p t n", t=2)
        pnum = bank[3][:, :].rearrange("p (t n) -> p t n", t=2)
        poT = bank[4][:, 0:S]
        py = bank[5][:, 0:S].rearrange("p (t n) -> p t n", t=2)
        pkk = bank[6][:, 0:D + HEADS]
        px1T = [bank[4][:, S:2 * S], bank[2][:, S:2 * S]]
        pc = bank[7][:, 0:P].rearrange("p (t b c) -> p t b c", t=2, b=B)
        pkf = bank[7][:, P:2 * P].rearrange("p (a n) -> p a n", a=2)
        pqf = bank[1][:, 0:P].rearrange("p (a n) -> p a n", a=2)
        pcorr = bank[3][:, 0:S]
        prT = bank[4][:, 0:P].rearrange("p (h n) -> p h n", h=2)
        pO = [bank[6][:, :].rearrange("p (b n) -> p b n", b=4), bank[7][:, :].rearrange("p (b n) -> p b n", b=4)]
        plg = bank[2][:, 0:P].rearrange("p (t e) -> p t e", e=E)
        ppos = bank[2][:, P:2 * P].rearrange("p (t e) -> p t e", e=E)
        pidx = bank[2][:, 2 * P:2 * P + NI]
        pT = bank[5]
        pH = [bank[0], bank[1], bank[3], bank[4]]
        pY = [bank[6][:, :].rearrange("p (t n) -> p t n", n=D), bank[7][:, :].rearrange("p (t n) -> p t n", n=D)]

        ld_w = sem("ld_w")
        ld_w2 = sem("ld_w2")
        ld_vec = sem("ld_vec")
        ld_tab = sem("ld_tab")
        ld_xT = [sem(f"ld_xT{i}") for i in range(4)]
        ld_x = sem("ld_x")
        ld_ctx = sem("ld_ctx")
        ld_dft = sem("ld_dft")
        ld_moe = sem("ld_moe")
        zero_set = sem("zero_set")
        acc_zeroed = sem("acc_zeroed")
        consts_set = sem("consts_set")
        xe_set = sem("xe_set")
        ones_set = sem("ones_set")
        xbias = sem("xbias")
        dve_o = sem("dve_o")
        act_o = sem("act_o")
        pool_o = sem("pool_o")
        qk_raw = sem("qk_raw")
        qk_parts = sem("qk_parts")
        qk_phi = sem("qk_phi")
        v_raw = sem("v_raw")
        v_biased = sem("v_biased")
        kT_raw = sem("kT_raw")
        kT_copied = sem("kT_copied")
        kk_raw = sem("kk_raw")
        kk_masked = sem("kk_masked")
        num_raw = sem("num_raw")
        o_ready = sem("o_ready")
        oT_raw = sem("oT_raw")
        oT_copied = sem("oT_copied")
        y_raw = sem("y_raw")
        y_summed = sem("y_summed")
        norm1_ready = sem("norm1_ready")
        x1_dve = sem("x1_dve")
        x1_pool = sem("x1_pool")
        x1_biased = sem("x1_biased")
        x1T_raw = sem("x1T_raw")
        x1T_copied = sem("x1T_copied")
        kc_raw = sem("kc_raw")
        kc_ready = sem("kc_ready")
        kf_raw = sem("kf_raw")
        kf_ready = sem("kf_ready")
        qc_raw = sem("qc_raw")
        qc_ready = sem("qc_ready")
        qf_raw = sem("qf_raw")
        spec_ready = sem("spec_ready")
        corr_raw = sem("corr_raw")
        top_ready = sem("top_ready")
        c_exp = sem("c_exp")
        xf_ready = sem("xf_ready")
        rT_raw = sem("rT_raw")
        rT_copied = sem("rT_copied")
        O_raw = sem("O_raw")
        norm2_ready = sem("norm2_ready")
        x2_dve = sem("x2_dve")
        x2_act = sem("x2_act")
        x2T_raw = sem("x2T_raw")
        x2T_copied = sem("x2T_copied")
        lg_raw = sem("lg_raw")
        pair_ready = sem("pair_ready")
        pos_raw = sem("pos_raw")
        diff_ready = sem("diff_ready")
        gate_exp = sem("gate_exp")
        gates_ready = sem("gates_ready")
        onehots = sem("onehots")
        slots_ready = sem("slots_ready")
        idx_raw = sem("idx_raw")
        idx_ready = sem("idx_ready")
        rows_out = sem("rows_out")
        gathered = [sem(f"gathered{e}") for e in range(SPARSE)]
        added = sem("added")
        xeT_raw = sem("xeT_raw")
        xeT_copied = sem("xeT_copied")
        h_raw = sem("h_raw")
        h_gelu = sem("h_gelu")
        h_ready = sem("h_ready")
        ye_raw = sem("ye_raw")
        ye_taken = sem("ye_taken")
        ld_acc = [sem(f"ld_acc{g}") for g in range(4)]
        norm3_ready = sem("norm3_ready")
        out_dve = sem("out_dve")
        out_act = sem("out_act")
        out_stored = sem("out_stored")

        dense, sparse = units()
        every = dense + sparse
        DLAG = 3

        def sparse_unit(u):
            return u - len(dense)

        block = ctx.enter_context(nc.Block())

        @block.sync
        def _(sp):
            sp.dma_start(xT[:, 0:512], xt[:, 0:512]).then_inc(ld_xT[0], 16)
            sp.dma_start(W[:, 0:W_O], weights[:, 0:W_O]).then_inc(ld_w, 16)
            sp.dma_start(vec[:, :], vectors.partition_broadcast(P)).then_inc(ld_vec, 16)
            sp.dma_start(tab[:, :], tables).then_inc(ld_tab, 16)
            sp.dma_start(x[:, :, :], xr.rearrange("(t p) d -> p t d", p=P)).then_inc(ld_x, 16)
            for i in range(1, 4):
                sp.dma_start(xT[:, 512 * i:512 * (i + 1)], xt[:, 512 * i:512 * (i + 1)]).then_inc(ld_xT[i], 16)
            sp.dma_start(W[:, W_O:], weights[:, W_O:]).then_inc(ld_w2, 16)
            sp.dma_start(ctxT[:, :], ctxt).then_inc(ld_ctx, 16)
            sp.dma_start(fwd[:, :, :], dft).then_inc(ld_dft, 16)
            sp.dma_start(inv[:, :, :], idft).then_inc(ld_dft, 16)
            sp.dma_start(W1[:, :, :], w1.rearrange("e d f -> d e f")).then_inc(ld_moe, 16)
            sp.dma_start(W2[:, :, :, :], w2.rearrange("e (c f) d -> f e c d", f=P)).then_inc(ld_moe, 16)
            sp.wait_ge(zero_set, 1)
            for g in range(4):
                sp.dma_start(acc_d.rearrange("(g p t) d -> g p (t d)", g=4, p=P)[g], zero[:, :]).then_inc(acc_zeroed, 16)
            sp.wait_ge(gates_ready, 1)
            sp.dma_start(rows_d.rearrange("(t p) d -> p t d", p=P), x2g[:, :, :]).then_inc(rows_out, 16)
            sp.wait_ge(added, 16 * NBLK * SPARSE)
            for g in range(4):
                sp.dma_start(acc[:, 4 * g:4 * g + 4, :],
                             acc_d[512 * g:512 * (g + 1), :].rearrange("(t p) d -> p t d", p=P)).then_inc(ld_acc[g], 16)
            for g in range(4):
                sp.wait_ge(out_dve, g + 1)
                sp.wait_ge(out_act, g + 1)
                sp.dma_start(out[512 * g:512 * (g + 1), :].rearrange("(t p) d -> p t d", p=P),
                             res[:, 4 * g:4 * g + 4, :]).then_inc(out_stored, 16)
            sp.wait_ge(out_stored, 64)

        @block.tensor
        def _(pe):
            def project_qk(b):
                pe.wait_ge(ld_xT[b // 2], 16)
                if b >= 1:
                    pe.wait_ge(qk_parts, 4 * b)
                for a, w in ((0, W_Q), (1, W_K)):
                    last = nc.tensor.matmul(pqk[:, a, :], W[:, w:w + D], xT[:, S * b:S * (b + 1)], start=True, stop=True)
                last.then_inc(qk_raw, 1)

            def project_v(b):
                if b >= 1:
                    pe.wait_ge(v_biased, b)
                for t in range(2):
                    j = 2 * b + t
                    last = nc.tensor.matmul(pv[:, t, :], xT[:, P * j:P * (j + 1)], W[:, W_V:W_V + D],
                                            start=True, stop=True)
                last.then_inc(v_raw, 1)

            def turn_k(b):
                pe.wait_ge(qk_phi, b + 1)
                if b == 0:
                    pe.wait_ge(ld_tab, 16)
                if b >= 1:
                    pe.wait_ge(kT_copied, b)
                for t in range(2):
                    last = nc.tensor.transpose(pkT[:, t, :], phi[:, b % 2, 1, P * t:P * (t + 1)], ident)
                last.then_inc(kT_raw, 1)

            def keys_values(b):
                pe.wait_ge(kT_copied, b + 1)
                pe.wait_ge(v_biased, b + 1)
                if b == 0:
                    pe.wait_ge(ones_set, 1)
                if b >= 1:
                    pe.wait_ge(kk_masked, b)
                for t in range(2):
                    last = nc.tensor.matmul(pkk, kphi[:, b % 2, t, :], v[:, b % 2, t, :],
                                            start=(t == 0), stop=(t == 1))
                last.then_inc(kk_raw, 1)

            def attend(b):
                pe.wait_ge(kk_masked, b + 1)
                if b >= 1:
                    pe.wait_ge(o_ready, b)
                for t in range(2):
                    last = nc.tensor.matmul(pnum[:, t, 0:D + HEADS], phi[:, b % 2, 0, P * t:P * (t + 1)],
                                            kvm[:, b % 2, :], start=True, stop=True)
                last.then_inc(num_raw, 1)

            def turn_o(b):
                pe.wait_ge(o_ready, b + 1)
                if b >= 1:
                    pe.wait_ge(oT_copied, b)
                for t in range(2):
                    last = nc.tensor.transpose(poT[:, P * t:P * (t + 1)], o[:, b % 2, t, :], ident)
                last.then_inc(oT_raw, 1)

            def project_o(b):
                pe.wait_ge(oT_copied, b + 1)
                if b == 0:
                    pe.wait_ge(ld_w2, 16)
                if b >= 1:
                    pe.wait_ge(y_summed, b)
                for t in range(2):
                    last = nc.tensor.matmul(py[:, t, :], oT[:, b % 2, P * t:P * (t + 1)], W[:, W_O:W_O + D],
                                            start=True, stop=True)
                last.then_inc(y_raw, 1)

            def project_ctx(b):
                if b == 0:
                    pe.wait_ge(ld_ctx, 16)
                    pe.wait_ge(ld_w2, 16)
                for t in range(2):
                    j = 2 * b + t
                    last = nc.tensor.matmul(pc[:, t, b, :], ctxT[:, P * j:P * (j + 1)], W[:, W_XQ:W_XQ + XC],
                                            start=True, stop=True)
                last.then_inc(kc_raw, 1)

            def spectrum(into, of):
                for a in range(2):
                    for t in range(2):
                        last = nc.tensor.matmul(into[:, a, :], fwd[:, t, P * a:P * (a + 1)], of[:, t, :],
                                                start=(t == 0), stop=(t == 1))
                return last

            def turn_x1(b):
                pe.wait_ge(x1_dve, b // 2 + 1)
                if b % 2:
                    pe.wait_ge(x1_pool, b // 2 + 1)
                if b >= 2:
                    pe.wait_ge(x1T_copied, b - 1)
                pe.wait_ge(kT_copied if b % 2 else oT_copied, B)
                for t in range(2):
                    last = nc.tensor.transpose(px1T[b % 2][:, P * t:P * (t + 1)], x1[:, 2 * b + t, :], ident)
                last.then_inc(x1T_raw, 1)

            def project_x1(b):
                pe.wait_ge(x1T_copied, b + 1)
                if b == 0:
                    pe.wait_ge(kf_ready, 1)
                for t in range(2):
                    last = nc.tensor.matmul(pc[:, t, b, :], x1T[:, b % 2, P * t:P * (t + 1)], W[:, W_XQ:W_XQ + XC],
                                            start=True, stop=True)
                last.then_inc(qc_raw, 1)

            pe.wait_ge(ld_w, 16)
            for i in range(ROUNDS):
                if i < B:
                    project_qk(i)
                if 1 <= i <= B:
                    turn_k(i - 1)
                if 2 <= i <= B + 1:
                    attend(i - 2)
                if i < B:
                    project_v(i)
                if 1 <= i <= B:
                    keys_values(i - 1)
                if 3 <= i <= 6:
                    project_ctx(2 * i - 6)
                    project_ctx(2 * i - 5)
                if 3 <= i <= B + 2:
                    project_o(i - 3)
                if 2 <= i <= B + 1:
                    turn_o(i - 2)
                if i == 8:
                    pe.wait_ge(kc_ready, 1)
                    pe.wait_ge(ld_dft, 32)
                    spectrum(pkf, kc).then_inc(kf_raw, 1)
                for b in range(B):
                    if ROUND_X1[b] == i:
                        turn_x1(b)
                for b in range(B):
                    if ROUND_X1[b] == i:
                        project_x1(b)

            pe.wait_ge(qc_ready, 1)
            spectrum(pqf, qc).then_inc(qf_raw, 1)
            pe.wait_ge(spec_ready, 1)
            nc.tensor.matmul(pcorr, s1[:, 0:1].broadcast_to([P, P]), inv[:, 0, :], start=True, stop=False)
            nc.tensor.matmul(pcorr, s2[:, 0:1].broadcast_to([P, P]), inv[:, 1, :], start=False, stop=True).then_inc(corr_raw, 1)
            pe.wait_ge(xf_ready, 1)
            for h in range(2):
                for a in range(2):
                    last = nc.tensor.matmul(prT[:, h, :], inv[:, a, P * h:P * (h + 1)], xf[:, a, :],
                                            start=(a == 0), stop=(a == 1))
            last.then_inc(rT_raw, 1)
            for b in range(B):
                if b % 4 == 0:
                    pe.wait_ge(rT_copied, b // 4 + 1)
                last = nc.tensor.matmul(pO[b // 4][:, b % 4, :], rTw[:, b, :, :].rearrange("p n k -> p (n k)"),
                                        W[:, W_XO:W_XO + D], start=True, stop=True)
                if b % 4 == 3:
                    last.then_inc(O_raw, 1)

            def turn_x2(g):
                pe.wait_ge(x2_dve, g + 1)
                pe.wait_ge(x2_act, g + 1)
                if g >= 1:
                    pe.wait_ge(x2T_copied, g)
                for t in range(4):
                    last = nc.tensor.transpose(pT[:, P * t:P * (t + 1)], x2g[:, 4 * g + t, 0:D], ident)
                last.then_inc(x2T_raw, 1)

            def logits(g):
                pe.wait_ge(x2T_copied, g + 1)
                for t in range(4):
                    j = 4 * g + t
                    last = nc.tensor.matmul(plg[:, j, :], x2T[:, P * j:P * (j + 1)], W[:, W_G:W_G + E],
                                            start=True, stop=True)
                last.then_inc(lg_raw, 1)

            def up(u):
                e, t0, n = every[u]
                if u == 0:
                    pe.wait_ge(ld_moe, 32)
                rhs = x2T[:, P * t0:P * (t0 + n)] if u < len(dense) else xeT[:, u % 2, 0:P * n]
                for f, h in enumerate((0, 2, 1, 3)):
                    if u >= 1:
                        pe.wait_ge(h_gelu if h < 2 else h_ready, 2 * u - 1 + h % 2)
                    nc.tensor.matmul(pH[h][:, 0:P * n], W1[:, e, P * h:P * (h + 1)], rhs,
                                     start=True, stop=True).then_inc(h_raw, 1)

            def down(u):
                e, t0, n = every[u]
                pe.wait_ge(h_ready, 2 * (u + 1))
                if u >= 2:
                    pe.wait_ge(ye_taken, u - 1)
                for t in range(n):
                    for c in range(2):
                        last = nc.tensor.matmul(pY[u % 2][:, t, :], hT[:, u % NH, c, P * t:P * (t + 1)], W2[:, e, c, :],
                                                start=(c == 0), stop=(c == 1))
                last.then_inc(ye_raw, 1)

            def turn_xe(u):
                s = sparse_unit(u)
                e, b0, n = every[u]
                pe.wait_ge(gathered[e - DENSE], 16 * NBLK)
                if s >= 1:
                    pe.wait_ge(xeT_copied, s)
                for t in range(n):
                    last = nc.tensor.transpose(pT[:, P * t:P * (t + 1)], xe[:, e - DENSE, b0 + t, 0:D], ident)
                last.then_inc(xeT_raw, 1)

            for g in range(4):
                turn_x2(g)
                logits(g)
            for u in range(len(dense)):
                if u == 2:
                    pe.wait_ge(pair_ready, 1)
                    nc.tensor.matmul(ppos, tri16[:, :], m16[:, :, :], start=True, stop=False, skip_group_check=True)
                    for i in range(NT - 1):
                        last = nc.tensor.matmul(ppos[:, i + 1:, :], ones16[:, :],
                                                m16[:, i:i + 1, :].broadcast_to([P, NT - 1 - i, E]),
                                                start=False, stop=(i == NT - 2), skip_group_check=True)
                    last.then_inc(pos_raw, 1)
                if u == 5:
                    pe.wait_ge(onehots, 1)
                    for i in range(2 * NT):
                        last = nc.tensor.matmul(pidx, ohl[:, i, :], ohb[:, i, :], start=(i == 0), stop=(i == 2 * NT - 1))
                    last.then_inc(idx_raw, 1)
                up(u)
                if u >= DLAG:
                    down(u - DLAG)
            for u in range(len(dense) - DLAG, len(dense)):
                down(u)
            n = len(dense)
            turn_xe(n)
            for u in range(n, len(every)):
                pe.wait_ge(xeT_copied, sparse_unit(u) + 1)
                up(u)
                if u + 1 < len(every):
                    turn_xe(u + 1)
                if u > n:
                    down(u - 1)
            down(len(every) - 1)

        @block.scalar
        def _(act):
            def qk_part(b, a):
                act.wait_ge(qk_raw, b + 1)
                if b >= 2:
                    act.wait_ge(qk_phi, b - 1)
                bias = W[:, W_BQ + a:W_BQ + a + 1]
                nc.scalar.activation(qke[:, b % 2, a, :], pqk[:, a, :], ACT.Exp, bias=bias).then_inc(qk_parts, 1)
                nc.scalar.activation(qkr[:, b % 2, a, :], pqk[:, a, :], ACT.Relu, bias=bias).then_inc(qk_parts, 1)

            def copy_kT(b):
                act.wait_ge(kT_raw, b + 1)
                if b >= 2:
                    act.wait_ge(kk_raw, b - 1)
                nc.scalar.activation(kphi[:, b % 2, :, :], pkT, ACT.Copy).then_inc(kT_copied, 1)

            def copy_oT(b):
                act.wait_ge(oT_raw, b + 1)
                if b >= 2:
                    act.wait_ge(y_raw, b - 1)
                nc.scalar.activation(oT[:, b % 2, :], poT, ACT.Copy).then_inc(oT_copied, 1)

            def copy_x1T(b):
                act.wait_ge(x1T_raw, b + 1)
                if b >= 2:
                    act.wait_ge(qc_raw, b - 1)
                nc.scalar.activation(x1T[:, b % 2, :], px1T[b % 2], ACT.Copy).then_inc(x1T_copied, 1)

            act.wait_ge(ld_w, 16)
            for i in range(ROUNDS):
                if i < B:
                    qk_part(i, 0)
                if 1 <= i <= B:
                    copy_kT(i - 1)
                if i < B:
                    qk_part(i, 1)
                if 2 <= i <= B + 1:
                    copy_oT(i - 2)
                for b in range(B):
                    if ROUND_X1[b] == i:
                        copy_x1T(b)
            act.wait_ge(top_ready, 1)
            nc.scalar.activation(cexp[:, :], pcorr, ACT.Exp, bias=ntop[:, 0:1]).then_inc(c_exp, 1)

            def norm(to, g, count, done):
                act.wait_ge(count, g // 2 + 1)
                for t in (4 * g + 2, 4 * g + 3):
                    last = nc.scalar.activation(to(t), r[:, t, :], ACT.Identity, scale=rs[:, t:t + 1], bias=nmr[:, t:t + 1])
                last.then_inc(done, 1)

            def copy_x2T(g):
                act.wait_ge(x2T_raw, g + 1)
                nc.scalar.activation(x2T[:, 512 * g:512 * (g + 1)], pT[:, :], ACT.Copy).then_inc(x2T_copied, 1)

            norm(lambda t: x2g[:, t, 0:D], 0, norm2_ready, x2_act)
            norm(lambda t: x2g[:, t, 0:D], 1, norm2_ready, x2_act)
            copy_x2T(0)
            copy_x2T(1)
            norm(lambda t: x2g[:, t, 0:D], 2, norm2_ready, x2_act)
            norm(lambda t: x2g[:, t, 0:D], 3, norm2_ready, x2_act)
            copy_x2T(2)
            copy_x2T(3)
            act.wait_ge(diff_ready, 1)
            nc.scalar.activation(ge[:, :], gd[:, :], ACT.Exp).then_inc(gate_exp, 1)

            def gelu(u):
                e, t0, n = every[u]
                for c in range(2):
                    act.wait_ge(h_raw, 4 * u + (1 if c == 0 else 3))
                    if u >= 1:
                        act.wait_ge(h_ready, 2 * u - 1 + c)
                    nc.scalar.activation(gel[:, c, 0:P * n], pH[c][:, 0:P * n], ACT.Gelu).then_inc(h_gelu, 1)

            def copy_xe(u):
                s = sparse_unit(u)
                e, b0, n = every[u]
                act.wait_ge(xeT_raw, s + 1)
                if s >= 2:
                    act.wait_ge(h_raw, 4 * (u - 1))
                nc.scalar.activation(xeT[:, u % 2, 0:P * n], pT[:, 0:P * n], ACT.Copy).then_inc(xeT_copied, 1)

            for u in range(len(dense)):
                gelu(u)
            n = len(dense)
            copy_xe(n)
            for u in range(n, len(every)):
                gelu(u)
                if u + 1 < len(every):
                    copy_xe(u + 1)
            for g in range(4):
                norm(lambda t: res[:, t, :], g, norm3_ready, out_act)

        @block.gpsimd
        def _(pool):
            order = Order(pool, pool_o)
            nc.gpsimd.memset(v[:, :, :, D:], 1.0).then_inc(ones_set, 1)
            nc.gpsimd.memset(zero[:, :], 0.0).then_inc(zero_set, 1)
            nc.gpsimd.memset(ones16[:, :], 1.0).then_inc(consts_set, 1)
            nc.gpsimd.memset(xe[:, :, :, :], 0.0).then_inc(xe_set, 1)

            def bias_x(b):
                j = 2 * b
                nc.gpsimd.tensor_tensor(x[:, j:j + 2, :], x[:, j:j + 2, :],
                                        vec[:, V_O:V_O + D].unsqueeze(1).broadcast_to([P, 2, D]), ALU.add).then_inc(xbias, 1)

            def bias_x1(b):
                pool.wait_ge(x1T_raw, b + 1)
                j = 2 * b
                nc.gpsimd.tensor_tensor(x1[:, j:j + 2, :], x1[:, j:j + 2, :],
                                        vec[:, V_XO:V_XO + D].unsqueeze(1).broadcast_to([P, 2, D]), ALU.add).then_inc(x1_biased, 1)

            def norm1(g):
                t = 4 * g + 3
                pool.wait_ge(norm1_ready, g + 1)
                nc.gpsimd.tensor_scalar(x1[:, t, :], r[:, t, :], mv[:, t, 0:1], rs[:, t:t + 1],
                                        ALU.subtract, ALU.mult).then_inc(x1_pool, 1)

            pool.wait_ge(ld_x, 16)
            pool.wait_ge(ld_vec, 16)
            for b in range(B):
                bias_x(b)
            norm1(0)
            norm1(1)
            for g in range(2):
                bias_x1(2 * g)
                bias_x1(2 * g + 1)
                norm1(g + 2)
            for b in range(4, B):
                bias_x1(b)

            def gather(s):
                for b in range(NBLK):
                    i = s * NBLK + b
                    nc.gpsimd.indirect_dma_start(
                        xe[:, s, b, :], None, rows_d[:, :],
                        bass.IndirectOffsetOnAxis(ap=idx[:, i:i + 1], axis=0),
                        bounds_check=N - 1, oob_is_err=False).then_inc(gathered[s], 16)

            def add_rows(s):
                pool.wait_ge(ye_taken, len(dense) + 2 * (s + 1))
                if s >= 1:
                    pool.wait_ge(added, 16 * NBLK * s)
                for b in range(NBLK):
                    i = s * NBLK + b
                    nc.gpsimd.indirect_dma_start(
                        acc_d[:, :], bass.IndirectOffsetOnAxis(ap=idx[:, i:i + 1], axis=0),
                        ye[:, s, b, :], None, bounds_check=N - 1, oob_is_err=False,
                        compute_op=ALU.add).then_inc(added, 16)

            pool.wait_ge(xe_set, 1)
            pool.wait_ge(idx_ready, 1)
            pool.wait_ge(rows_out, 16)
            pool.wait_ge(acc_zeroed, 64)
            gather(0)
            gather(1)
            for s in range(SPARSE):
                if s + 2 < SPARSE:
                    gather(s + 2)
                add_rows(s)

        @block.vector
        def _(dve):
            order = Order(dve, dve_o)
            tt, ts, stt = nc.vector.tensor_tensor, nc.vector.tensor_scalar, nc.vector.scalar_tensor_tensor

            def bias_v(b):
                dve.wait_ge(v_raw, b + 1)
                if b >= 2:
                    dve.wait_ge(kk_raw, b - 1)
                tt(v[:, b % 2, :, 0:D], pv, vec[:, V_V:V_V + D].unsqueeze(1).broadcast_to([P, 2, D]),
                   ALU.add).then_inc(v_biased, 1)

            def phi_qk(b):
                dve.wait_ge(qk_parts, 4 * (b + 1))
                if b >= 2:
                    dve.wait_ge(kT_raw, b - 1)
                    dve.wait_ge(num_raw, b - 1)
                stt(phi[:, b % 2, :, :], qke[:, b % 2, :, :], 1.0, qkr[:, b % 2, :, :], ALU.min, ALU.add).then_inc(qk_phi, 1)

            def mask_kk(b):
                dve.wait_ge(kk_raw, b + 1)
                if b == 0:
                    dve.wait_ge(ld_tab, 16)
                if b >= 2:
                    dve.wait_ge(num_raw, b - 1)
                tt(kvm[:, b % 2, 0:D], pkk[:, 0:D], tab[:, T_HEAD:T_HEAD + D], ALU.mult)
                stt(kvm[:, b % 2, D:], pkk[:, D:], ATT_EPS, tab[:, T_HEAD + D:T_HEAD + D + HEADS],
                    ALU.add, ALU.mult).then_inc(kk_masked, 1)

            def normaliser(b):
                dve.wait_ge(num_raw, b + 1)
                return order.mark(ts(z0[:, :, :], pnum[:, :, D:D + HEADS], ATT_EPS, None, ALU.add))

            def normaliser_inverse(after):
                order.wait(after)
                return order.mark(nc.vector.reciprocal(z1[:, :, :], z0[:, :, :]))

            def normalise(b, after):
                if b >= 2:
                    dve.wait_ge(oT_raw, b - 1)
                order.wait(after)
                tt(o[:, b % 2, :, :].rearrange("p t (h c) -> p t h c", c=DK),
                   pnum[:, :, 0:D].rearrange("p t (h c) -> p t h c", c=DK),
                   z1[:, :, :].unsqueeze(3).broadcast_to([P, 2, HEADS, DK]), ALU.mult).then_inc(o_ready, 1)

            def residual1(b):
                dve.wait_ge(y_raw, b + 1)
                dve.wait_ge(xbias, b + 1)
                j = 2 * b
                tt(r[:, j:j + 2, :], py, x[:, j:j + 2, :], ALU.add).then_inc(y_summed, 1)

            def statistics(t0, t1, count, n):
                dve.wait_ge(count, n)
                for t in range(t0, t1):
                    last = nc.vector.bn_stats(stats[:, t, :], r[:, t, :])
                return order.mark(last)

            def moments(t0, t1, after):
                order.wait(after)
                for t in range(t0, t1):
                    last = nc.vector.bn_aggr(mv[:, t, :], stats[:, t, :])
                return order.mark(last)

            def rsqrt_step(k, t0, t1, after, done=None):
                v, h, y, a = var[:, t0:t1], half[:, t0:t1], rs[:, t0:t1], ra[:, t0:t1]
                order.wait(after)
                if k == 0:
                    ins = ts(v, mv[:, t0:t1, 1:2].rearrange("p t o -> p (t o)"), LN_EPS, None, ALU.add)
                elif k == 1:
                    ins = ts(h, v.bitcast(I32), 1, None, ALU.logical_shift_right)
                elif k == 2:
                    ins = ts(y.bitcast(I32), h, -1.0, RSQRT_SEED, ALU.mult, ALU.add)
                elif k == 3:
                    ins = stt(a, y, -RSQRT_A, y, ALU.mult, ALU.mult)
                elif k == 5:
                    ins = stt(y, a, RSQRT_B, y, ALU.add, ALU.mult)
                elif k == 6:
                    ins = stt(a, y, -0.5, y, ALU.mult, ALU.mult)
                elif k == 8:
                    ins = stt(y, a, 1.5000003, y, ALU.add, ALU.mult)
                else:
                    ins = tt(a, a, v, ALU.mult)
                if done:
                    ins.then_inc(done, 1)
                    return None
                return order.mark(ins)

            def shift(t0, t1, after):
                order.wait(after)
                return stt(nmr[:, t0:t1], mv[:, t0:t1, 0:1].rearrange("p t o -> p (t o)"), -1.0, rs[:, t0:t1],
                           ALU.mult, ALU.mult)

            def apply_norm(to, t):
                return ts(to(t), r[:, t, :], mv[:, t, 0:1], rs[:, t:t + 1], ALU.subtract, ALU.mult)

            def prepare_k():
                dve.wait_ge(kf_raw, 1)
                order.done(nc.vector.tensor_copy(kf[:, :, :], pkf))
                c = [tab[:, T_SCALE + i:T_SCALE + i + 1] for i in range(8)]
                ka, kb = kf[:, 0, :], kf[:, 1, :]
                ts(k1[:, 0, :], ka, c[0], None, ALU.mult)
                ts(k1[:, 1, :], kb, c[1], None, ALU.mult)
                ts(k2[:, 0, :], kb, c[2], None, ALU.mult)
                ts(k2[:, 1, :], ka, c[1], None, ALU.mult)
                ts(va[:, 0, :], ka, c[4], None, ALU.mult)
                ts(va[:, 1, :], kb, c[5], None, ALU.mult)
                ts(vb[:, 0, :], kb, c[5], None, ALU.mult)
                order.done(ts(vb[:, 1, :], ka, c[6], None, ALU.mult))
                stt(k2[:, 1, :], kb, c[3], k2[:, 1, :], ALU.mult, ALU.add)
                ins = stt(vb[:, 1, :], kb, c[7], vb[:, 1, :], ALU.mult, ALU.add)
                ins.then_inc(kf_ready, 1)

            dve.wait_ge(ld_vec, 16)
            stats_n, rs_n = 0, 0
            for i in range(ROUNDS - 1):
                begin = i >= 5 and i % 2 == 1
                end = i >= 6 and i % 2 == 0
                g0 = 4 * ((i - 5) // 2)

                def step(k):
                    return rsqrt_step(k, g0, g0 + 4, rs_n)

                if 2 <= i <= B + 1:
                    z_n = normaliser(i - 2)
                if end:
                    rs_n = step(4)
                if i < B:
                    bias_v(i)
                if end:
                    rs_n = step(5)
                if 2 <= i <= B + 1:
                    z_n = normaliser_inverse(z_n)
                if end:
                    rs_n = step(6)
                if 4 <= i <= B + 3:
                    rs_n2 = moments(2 * (i - 4), 2 * (i - 4) + 2, stats_n)
                if end:
                    rs_n = step(7)
                if 2 <= i <= B + 1:
                    normalise(i - 2, z_n)
                if begin:
                    rs_n = rsqrt_step(0, g0, g0 + 4, rs_n2)
                if 1 <= i <= B:
                    mask_kk(i - 1)
                if end:
                    rsqrt_step(8, g0, g0 + 4, rs_n, norm1_ready)
                if begin:
                    rs_n = step(1)
                if 3 <= i <= B + 2:
                    residual1(i - 3)
                if begin:
                    rs_n = step(2)
                if end:
                    dve.wait_ge(norm1_ready, g0 // 4 + 1)
                    for t in range(g0, g0 + 3):
                        last = apply_norm(lambda t: x1[:, t, :], t)
                    last.then_inc(x1_dve, 1)
                if i < B:
                    phi_qk(i)
                if 3 <= i <= B + 2:
                    stats_n = statistics(2 * (i - 3), 2 * (i - 3) + 2, y_summed, i - 2)
                if begin:
                    rs_n = step(3)
                if i == 1:
                    nc.vector.tensor_copy(lane16[:, :], tab[:, T_LANE:T_LANE + P])
                    nc.vector.tensor_copy(tri16[:, :], tab[:, T_TRI:T_TRI + P]).then_inc(consts_set, 1)
                if i == 7:
                    dve.wait_ge(kc_raw, B)
                    tt(kc[:, :, :].rearrange("p t (b c) -> p t b c", c=XC), pc,
                       vec[:, V_XQ:V_XQ + XC].unsqueeze(1).unsqueeze(1).broadcast_to([P, 2, B, XC]), ALU.add).then_inc(kc_ready, 1)
                if i == 9:
                    prepare_k()

            dve.wait_ge(qc_raw, B)
            tt(qc[:, :, :].rearrange("p t (b c) -> p t b c", c=XC), pc,
               vec[:, V_XQ:V_XQ + XC].unsqueeze(1).unsqueeze(1).broadcast_to([P, 2, B, XC]), ALU.add).then_inc(qc_ready, 1)
            dve.wait_ge(qf_raw, 1)
            dve.wait_ge(kf_ready, 1)
            qf = pqf.rearrange("p a n -> p (a n)")
            order.done(nc.vector.tensor_tensor_reduce(
                out=junk[:, 0:P], in0=qf, in1=k1[:, :, :].rearrange("p a n -> p (a n)"), scale=1.0, scalar=0.0,
                op0=ALU.mult, op1=ALU.add, accum_out=s1[:, :]))
            nc.vector.tensor_tensor_reduce(
                out=junk[:, 0:P], in0=qf, in1=k2[:, :, :].rearrange("p a n -> p (a n)"), scale=1.0, scalar=0.0,
                op0=ALU.mult, op1=ALU.add, accum_out=s2[:, :]).then_inc(spec_ready, 1)
            dve.wait_ge(corr_raw, 1)
            order.done(nc.vector.max(top1[:, :], pcorr))
            order.done(nc.vector.match_replace(corr1[:, :], top1[:, :], pcorr, LOW))
            ts(ntop[:, :], top1[:, 0:1], -1.0, None, ALU.mult).then_inc(top_ready, 1)
            order.done(nc.vector.max(top2[:, :], corr1[:, :]))
            order.done(nc.vector.memset(top2[:, TOPK - 8:], LOW))
            order.done(nc.vector.match_replace(corr2[:, :], top2[:, :], corr1[:, :], LOW))
            dve.wait_ge(c_exp, 1)
            order.done(stt(cw[:, :], corr2[:, :], LOW, cexp[:, :], ALU.is_equal, ALU.mult, accum_out=csum[:, :]))
            order.done(nc.vector.reciprocal(crec[:, :], csum[:, :]))
            for a, w in ((0, wa), (1, wb)):
                order.done(nc.vector.tensor_tensor_reduce(
                    out=junk[:, :], in0=cw[:, :], in1=inv[:, a, :], scale=crec[:, 0:1], scalar=0.0,
                    op0=ALU.mult, op1=ALU.add, accum_out=w[:, :]))
            order.done(ts(xf[:, :, :], va[:, :, :], wa[:, 0:1], None, ALU.mult))
            stt(xf[:, :, :], vb[:, :, :], wb[:, 0:1], xf[:, :, :], ALU.mult, ALU.add).then_inc(xf_ready, 1)
            dve.wait_ge(rT_raw, 1)
            order.done(nc.vector.tensor_copy(rT[:, :, :].rearrange("p b (c h) -> p h b c", h=2),
                                             prT.rearrange("p h (b c) -> p h b c", c=XC)))
            for b in (0, 4):
                nc.vector.tensor_copy(rTw[:, b:b + 4, :, :],
                                      rT[:, b:b + 4, :].unsqueeze(2).broadcast_to([P, 4, P // 16, 16])).then_inc(rT_copied, 1)
            def residual2(b):
                if b % 4 == 0:
                    dve.wait_ge(O_raw, b // 4 + 1)
                dve.wait_ge(x1_biased, b + 1)
                j = 2 * b
                return order.mark(tt(r[:, j:j + 2, :], x1[:, j:j + 2, :],
                                     pO[b // 4][:, b % 4:b % 4 + 1, :].broadcast_to([P, 2, D]), ALU.add))

            def bn(t, after):
                order.wait(after)
                return order.mark(nc.vector.bn_stats(stats[:, t, :], r[:, t, :]))

            H = NT // 2
            sums = [residual2(b) for b in range(4)]
            for t in range(H):
                last = bn(t, sums[t // 2])
            n = moments(0, H, last)
            sums = []
            for k in range(RSQRT_OPS):
                n = rsqrt_step(k, 0, H, n)
                if k < 4:
                    sums.append(residual2(4 + k))
                else:
                    last = bn(H + k - 4, sums[(k - 4) // 2])
            shift(0, H, n).then_inc(norm2_ready, 1)
            for t in range(H + RSQRT_OPS - 4, NT):
                last = bn(t, sums[(t - H) // 2])
            for g in range(2):
                for t in (4 * g, 4 * g + 1):
                    ins = apply_norm(lambda t: x2g[:, t, 0:D], t)
                ins.then_inc(x2_dve, 1)
            n = moments(H, NT, last)
            for k in range(RSQRT_OPS):
                n = rsqrt_step(k, H, NT, n)
            shift(H, NT, n).then_inc(norm2_ready, 1)
            for g in range(2, 4):
                for t in (4 * g, 4 * g + 1):
                    ins = apply_norm(lambda t: x2g[:, t, 0:D], t)
                ins.then_inc(x2_dve, 1)

            def gating(u):
                e, t0, n = every[u]
                for c in range(2):
                    dve.wait_ge(h_gelu, 2 * u + 1 + c)
                    dve.wait_ge(h_raw, 4 * u + (2 if c == 0 else 4))
                    if u >= NH:
                        dve.wait_ge(ye_raw, u - NH + 1)
                    tt(hT[:, u % NH, c, 0:P * n], pH[2 + c][:, 0:P * n], gel[:, c, 0:P * n], ALU.mult).then_inc(h_ready, 1)

            def over_e(a):
                return a.unsqueeze(2).broadcast_to([P, NT, E])

            def route_experts():
                dve.wait_ge(lg_raw, 4)
                order.done(nc.vector.tensor_copy(lg[:, :, :], plg))
                for t in range(NT):
                    last = nc.vector.max(top[:, t, :], lg[:, t, :])
                order.done(last)
                for t in range(NT):
                    last = nc.vector.max_index(topi[:, t, :], top[:, t, :], lg[:, t, :])
                order.done(last)
                tt(gd[:, :], top[:, :, 1:2].rearrange("p t o -> p (t o)"), top[:, :, 0:1].rearrange("p t o -> p (t o)"),
                   ALU.subtract).then_inc(diff_ready, 1)
                order.done(nc.vector.tensor_copy(pick[:, :, :], topi[:, :, 0:2].rearrange("p t k -> p k t")))
                order.done(tt(oh[:, :, :, :].rearrange("p k t e -> p (k t) e"),
                              tab[:, T_EXP:T_EXP + E].unsqueeze(1).broadcast_to([P, 2 * NT, E]),
                              pick[:, :, :].rearrange("p k t -> p (k t)").unsqueeze(2).broadcast_to([P, 2 * NT, E]),
                              ALU.is_equal))
                tt(m16[:, :, :], oh[:, 0, :, :], oh[:, 1, :, :], ALU.add).then_inc(pair_ready, 1)

            def route_gates():
                dve.wait_ge(gate_exp, 1)
                order.done(ts(gs[:, :], ge[:, :], 1.0, None, ALU.add))
                order.done(nc.vector.reciprocal(g1[:, :], gs[:, :]))
                order.done(tt(g2[:, :], ge[:, :], g1[:, :], ALU.mult))
                tt(ga[:, :, :], oh[:, 0, :, :], over_e(g1[:, :]), ALU.mult)
                order.done(tt(gb[:, :, :], oh[:, 1, :, :], over_e(g2[:, :]), ALU.mult))
                order.done(tt(ga[:, :, :], ga[:, :, :], gb[:, :, :], ALU.add))
                dve.wait_ge(pos_raw, 1)
                stt(x2g[:, :, D:], ppos, float(CAP), ga[:, :, :], ALU.is_lt, ALU.mult).then_inc(gates_ready, 1)

            def route_slots():
                order.done(tt(sv[:, :, :], ppos, tab[:, T_SLOT:T_SLOT + E].unsqueeze(1).broadcast_to([P, NT, E]), ALU.add))
                order.done(ts(over[:, :, :], ppos, float(CAP), float(E * CAP * 2), ALU.is_ge, ALU.mult))
                order.done(tt(sv[:, :, :], sv[:, :, :], over[:, :, :], ALU.add))
                for k in range(2):
                    last = tt(ohs[:, k, :, :], oh[:, k, :, :], sv[:, :, :], ALU.mult)
                order.done(last)
                order.done(nc.vector.tensor_reduce(slot_f[:, :], ohs[:, :, :, :].rearrange("p k t e -> p (k t) e"), AX.X, ALU.add))
                order.done(nc.vector.tensor_copy(slot[:, :], slot_f[:, :]))
                ts(sblk[:, :], slot[:, :], 7, None, ALU.logical_shift_right)
                order.done(ts(slane_i[:, :], slot[:, :], P - 1, None, ALU.bitwise_and))
                order.done(nc.vector.tensor_copy(slane[:, :], slane_i[:, :]))

            def route_onehots(i0, i1):
                for i in range(i0, i1):
                    j = i % NT
                    last = ts(ohl[:, i, :], lane16[:, :], slane[:, i:i + 1], tab[:, T_TOK + j:T_TOK + j + 1],
                              ALU.is_equal, ALU.mult)
                if i1 == 2 * NT:
                    tt(ohb[:, :, :], tab[:, T_BLK + DENSE * NBLK:T_BLK + E * NBLK].unsqueeze(1).broadcast_to([P, 2 * NT, NI]),
                       sblk[:, :].unsqueeze(2).broadcast_to([P, 2 * NT, NI]), ALU.is_equal).then_inc(onehots, 1)

            def route_index():
                dve.wait_ge(idx_raw, 1)
                order.done(ts(idf[:, :], pidx, 0.0, float(4 * N), ALU.is_equal, ALU.mult))
                order.done(tt(idf[:, :], idf[:, :], pidx, ALU.add))
                ts(idx[:, :], idf[:, :], -1.0, None, ALU.add).then_inc(idx_ready, 1)

            def take_dense(u):
                e, t0, n = every[u]
                dve.wait_ge(ye_raw, u + 1)
                dve.wait_ge(gates_ready, 1)
                if u >= 1:
                    dve.wait_ge(ye_taken, u)
                for t in range(n):
                    j = t0 + t
                    base = x2g[:, j, 0:D] if e == 0 else dacc[:, j, :]
                    last = stt(dacc[:, j, :], pY[u % 2][:, t, :], x2g[:, j, D + e:D + e + 1], base, ALU.mult, ALU.add)
                last.then_inc(ye_taken, 1)

            def take_sparse(u):
                e, b0, n = every[u]
                s = e - DENSE
                dve.wait_ge(ye_raw, u + 1)
                tt(ye[:, s, b0:b0 + n, :], pY[u % 2][:, 0:n, :],
                   xe[:, s, b0:b0 + n, D + e:D + e + 1].broadcast_to([P, n, D]), ALU.mult).then_inc(ye_taken, 1)

            route_experts()
            gating(0)
            gating(1)
            route_gates()
            gating(2)
            route_slots()
            gating(3)
            route_onehots(0, 16)
            take_dense(0)
            gating(4)
            route_onehots(16, 32)
            take_dense(1)
            for u in range(5, len(dense)):
                gating(u)
                if u == 5:
                    route_index()
                take_dense(u - DLAG)
            for u in range(len(dense) - DLAG, len(dense)):
                take_dense(u)
            n = len(dense)
            for u in range(n, len(every)):
                gating(u)
                if u > n:
                    take_sparse(u - 1)
            take_sparse(len(every) - 1)
            def residual3(g):
                dve.wait_ge(ld_acc[g], 16)
                return order.mark(tt(r[:, 4 * g:4 * g + 4, :], dacc[:, 4 * g:4 * g + 4, :], acc[:, 4 * g:4 * g + 4, :], ALU.add))

            sums = [residual3(g) for g in range(2)]
            for t in range(H):
                last = bn(t, sums[t // 4])
            n = moments(0, H, last)
            sums = []
            for k in range(RSQRT_OPS):
                n = rsqrt_step(k, 0, H, n)
                if k < 2:
                    sums.append(residual3(2 + k))
                elif k < 8:
                    last = bn(H + k - 2, sums[(k - 2) // 4])
            shift(0, H, n).then_inc(norm3_ready, 1)
            for t in range(H + 6, NT):
                last = bn(t, sums[(t - H) // 4])
            for g in range(2):
                for t in (4 * g, 4 * g + 1):
                    ins = apply_norm(lambda t: res[:, t, :], t)
                ins.then_inc(out_dve, 1)
            n = moments(H, NT, last)
            for k in range(RSQRT_OPS):
                n = rsqrt_step(k, H, NT, n)
            shift(H, NT, n).then_inc(norm3_ready, 1)
            for g in range(2, 4):
                for t in (4 * g, 4 * g + 1):
                    ins = apply_norm(lambda t: res[:, t, :], t)
                ins.then_inc(out_dve, 1)


def kernel(x, ctx_1024, L0_attn_Wq, L0_attn_bq, L0_attn_Wk, L0_attn_bk, L0_attn_Wv, L0_attn_bv, L0_attn_Wo,
           L0_attn_bo, L0_xattn_Wq, L0_xattn_bq, L0_xattn_Wout, L0_xattn_bout, L0_ffn_Wg, L0_ffn_W1, L0_ffn_W2):
    import numpy as np
    import concourse.bacc as bacc
    from concourse.bass_utils import run_bass_kernel_spmd

    a = np.asarray
    xr = np.ascontiguousarray(a(x).reshape(N, D))
    weights = np.concatenate([a(L0_attn_Wq).T, a(L0_attn_Wk).T, a(L0_attn_bq).reshape(D, 1),
                              a(L0_attn_bk).reshape(D, 1), a(L0_attn_Wv).T,
                              a(L0_attn_Wo).T, a(L0_xattn_Wq), a(L0_xattn_Wout), a(L0_ffn_Wg).T], axis=1)
    vectors = np.concatenate([a(L0_attn_bv), a(L0_attn_bo), a(L0_xattn_bq), a(L0_xattn_bout)])

    p = np.arange(P)[:, None]
    tab = np.zeros((P, T_END), np.float32)
    tab[:, T_ID:T_ID + P] = np.eye(P)
    tab[:, T_HEAD:T_HEAD + D] = p // DK == np.arange(D)[None] // DK
    tab[:, T_HEAD + D:T_HEAD + D + HEADS] = p // DK == np.arange(HEADS)[None]
    scale = np.where(p[:, 0] == 0, 1.0, 2.0) / S
    rest = np.where(p[:, 0] == 0, 0.0, 1.0)
    mean = 1.0 / (B * XC)
    for i, c in enumerate([scale * mean, scale * rest * mean, -scale * rest * mean, scale * (1 - rest) * mean,
                           scale, scale * rest, -scale * rest, scale * (1 - rest)]):
        tab[:, T_SCALE + i] = c
    tab[:, T_EXP:T_EXP + E] = np.arange(E)
    tab[:, T_SLOT:T_SLOT + E] = CAP * np.arange(E)
    tab[:, T_BLK:T_BLK + E * NBLK] = np.arange(E * NBLK)
    tab[:, T_LANE:T_LANE + P] = np.arange(P)
    tab[:, T_TOK:T_TOK + NT] = p + P * np.arange(NT)[None] + 1
    tab[:, T_TRI:T_TRI + P] = p < np.arange(P)[None]
    time, turn = np.arange(S)[:, None], np.arange(P)[None]
    angle = 2 * np.pi * ((time * turn) % S) / S
    basis = np.concatenate([np.cos(angle), np.sin(angle)], axis=1)
    basis[:, P] = 1 - 2 * (np.arange(S) % 2)
    dft = basis.reshape(2, P, S).transpose(1, 0, 2)
    idft = basis.T.reshape(2, P, S).transpose(1, 0, 2)

    arrays = {
        "xt": np.ascontiguousarray(xr.T), "xr": xr, "ctxt": np.ascontiguousarray(a(ctx_1024).reshape(N, D).T),
        "weights": np.ascontiguousarray(weights), "vectors": vectors, "tables": tab,
        "dft": np.ascontiguousarray(dft.astype(np.float32)), "idft": np.ascontiguousarray(idft.astype(np.float32)),
        "w1": np.ascontiguousarray(a(L0_ffn_W1)), "w2": np.ascontiguousarray(a(L0_ffn_W2)),
    }
    nc = bacc.Bacc("TRN2", target_bir_lowering=False, num_devices=1)
    args = [nc.dram_tensor(f"in_{name}", v.shape, mybir.dt.from_np(v.dtype), kind="ExternalInput").ap()
            for name, v in arrays.items()]
    out = nc.dram_tensor("out", (N, D), F32, kind="ExternalOutput").ap()
    decoder_layer(nc, *args, out)
    got = run_bass_kernel_spmd(nc, [{f"in_{name}": v for name, v in arrays.items()}], core_ids=[0])
    return got.results[0]["out"].reshape(B, S, D)
```

```python
from contextlib import ExitStack

import concourse.bass as bass
from concourse import mybir

F32 = mybir.dt.float32
F32R = mybir.dt.float32r
F16 = mybir.dt.float16
I32 = mybir.dt.int32
U32 = mybir.dt.uint32
ALU = mybir.AluOpType
ACT = mybir.ActivationFunctionType
AX = mybir.AxisListType

P = 128
B, S, D = 8, 256, 128
N = B * S
NT = N // P
HEADS, DK = 16, 8
XC = 8
TOPK = 11
E, K2 = 8, 2
FF = 256
CAP = N * K2 * 5 // 4 // E
NBLK = CAP // P
GROUPS = [(0, 4), (4, 4), (8, 8)]
DENSE = 2
SPARSE = E - DENSE
LN_EPS = 1e-5
ATT_EPS = 1e-6
ROW = D + E + 1
FAR = 8192
LOW = -3.0e38

W_Q, W_K, W_BQ, W_BK, W_V, W_O, W_XQ, W_XO, W_G, W_END = 0, 128, 256, 257, 258, 386, 514, 522, 650, 658
V_V, V_O, V_XQ, V_XO, V_END = 0, 128, 256, 264, 392
T_ID, T_HEAD, T_SCALE, T_EXP, T_SLOT, T_TOK, T_TRI, T_END = 0, 128, 272, 280, 288, 296, 312, 440

RSQRT_SEED = float(0x5F1FFFF9)
RSQRT_A, RSQRT_B = 0.703952253, 0.703952253 * 2.38924456
RSQRT_OPS = 9
ROUNDS = 14
NORM3_DVE = [1, 1, 2, 2]
NORM2_DVE = [2, 0, 3]
NORM1_DVE = [2, 2, 2, 4]
ROUND_CTX = [8, 8, 8, 9, 9, 9, 10, 10]
ROUND_X1 = [9, 9, 10, 10, 11, 11, 13, 13]


class Order:

    def __init__(self, eng, sem):
        self.eng, self.sem, self.n = eng, sem, 0

    def mark(self, ins):
        self.n += 1
        ins.then_inc(self.sem, 1)
        return self.n

    def wait(self, n):
        self.eng.wait_ge(self.sem, n)

    def done(self, ins):
        self.n += 1
        ins.then_inc(self.sem, 1)
        self.eng.wait_ge(self.sem, self.n)


def units():
    dense = [(e, 4 * g, 4) for g in range(NT // 4) for e in range(DENSE)]
    sparse = [(e, b0, n) for e in range(DENSE, E) for b0, n in ((0, 3), (3, 2))]
    return dense, sparse


def decoder_layer(nc, xt, xr, ctxt, weights, vectors, tables, dft, idft, w1, w2, out):
    ctx = ExitStack()
    with ctx:
        def sb(name, shape, dt=F32):
            return ctx.enter_context(nc.sbuf_tensor(name, shape, dt))

        def sem(name):
            return ctx.enter_context(nc.semaphore(name))

        slots_d = nc.dram_tensor("slots_d", [SPARSE * CAP, ROW], F32, kind="Internal").ap()
        sum_d = [nc.dram_tensor(f"sum_d{i}", [N, D], F32, kind="Internal").ap() for i in range(2)]

        xT = sb("xT", [P, N])
        x = sb("x", [P, NT, D])
        ctxT = sb("ctxT", [P, N])
        W = sb("W", [P, W_END])
        vec = sb("vec", [P, V_END])
        tab = sb("tab", [P, T_END])
        fwd = sb("fwd", [P, 2, S])
        inv = sb("inv", [P, 2, S])
        W1 = sb("W1", [P, E, 2 * FF])
        W1h = sb("W1h", [P, E, 2 * FF], F32R)
        W1l = sb("W1l", [P, E, 2 * FF], F32R)
        W2 = sb("W2", [P, E, 2, D])
        ident = tab[:, T_ID:T_ID + P]
        tri16 = sb("tri16", [P, P], F16)
        ones16 = sb("ones16", [P, P], F16)

        NH = 4
        hT = sb("hT", [P, NH, 2, 4 * P])
        v = sb("v", [P, 2, 2, D + HEADS])
        qke, qkr, phi = (hT[:, i, :, :].rearrange("p a (q s) -> p a q s", q=2) for i in range(3))
        kphi = sb("kphi", [P, 2, 2, D])
        kvm = sb("kvm", [P, 2, D + HEADS])
        z0 = sb("z0", [P, 2, HEADS])
        z1 = sb("z1", [P, 2, HEADS])
        o = sb("o", [P, 2, 2, D])
        oT = sb("oT", [P, 2, S])
        r = sb("r", [P, NT, D])
        stats = sb("stats", [P, NT, 6])
        mv = sb("mv", [P, NT, 2])
        var = sb("var", [P, NT])
        half = sb("half", [P, NT], I32)
        rs = sb("rs", [P, NT])
        ra = sb("ra", [P, NT])
        nmr = sb("nmr", [P, NT])
        x1 = sb("x1", [P, NT, D])
        x1T = sb("x1T", [P, 4, S])
        kc = sb("kc", [P, 2, B * XC])
        qc = sb("qc", [P, 2, B * XC])
        kf = sb("kf", [P, 2, B * XC])
        k1 = sb("k1", [P, 2, B * XC])
        k2 = sb("k2", [P, 2, B * XC])
        va = sb("va", [P, 2, B * XC])
        vb = sb("vb", [P, 2, B * XC])
        junk = sb("junk", [P, S])
        junk2 = sb("junk2", [P, S])
        s1 = sb("s1", [P, 1])
        s2 = sb("s2", [P, 1])
        top1 = sb("top1", [P, 8])
        top2 = sb("top2", [P, 8])
        ntop = sb("ntop", [P, 1])
        corr1 = sb("corr1", [P, S])
        corr2 = sb("corr2", [P, S])
        cexp = sb("cexp", [P, S])
        cw = sb("cw", [P, S])
        csum = sb("csum", [P, 1])
        crec = sb("crec", [P, 1])
        wa = sb("wa", [P, 1])
        wb = sb("wb", [P, 1])
        xf = sb("xf", [P, 2, B * XC])
        rT = sb("rT", [P, B, 16])
        rTw = sb("rTw", [P, B, P // 16, 16])
        H = NT // 2
        x2g = sb("x2g", [P, NT, ROW])
        x2T = xT
        x2Th = sb("x2Th", [P, 2, 4 * P], F32R)
        x2Tl = sb("x2Tl", [P, 2, 4 * P], F32R)
        lg = sb("lg", [P, NT, E])
        top = sb("top", [P, NT, 8])
        topi = sb("topi", [P, NT, 8], U32)
        pick = sb("pick", [P, NT, 2])
        oh = sb("oh", [P, NT, 2, E])
        m16 = sb("m16", [P, NT, E], F16)
        gd = sb("gd", [P, NT])
        th = sb("th", [P, NT])
        place = sb("place", [P, NT, E])
        pair = sb("pair", [P, NT, E])
        side = sb("side", [P, NT, E])
        gate = sb("gate", [P, NT, E])
        sv = sb("sv", [P, NT, E])
        over = sb("over", [P, NT, E])
        ohs = sb("ohs", [P, NT, 2, E])
        slot_f = sb("slot_f", [P, NT, 2])
        slot = sb("slot", [P, NT, 2], U32)
        xe = sb("xe", [P, SPARSE, NBLK, ROW])
        idx = sb("idx", [P, SPARSE, NBLK], U32)
        xeTh = sb("xeTh", [P, 2, 3 * P], F32R)
        xeTl = sb("xeTl", [P, 2, 3 * P], F32R)
        gel = sb("gel", [P, 2, 4 * P])
        ye = [y[:, :, :].rearrange("p t d -> p (t d)")[:, 0:SPARSE // 2 * NBLK * D].rearrange(
            "p (s b d) -> p s b d", s=SPARSE // 2, b=NBLK) for y in (x, x1)]
        dacc = r
        sum0 = ctxT[:, :].rearrange("p (t d) -> p t d", d=D)
        sum1 = x2g[:, :, 0:D]
        res = xT[:, :].rearrange("p (t d) -> p t d", d=D)

        bank = [ctx.enter_context(nc.psum_tensor(f"bank{i}", [P, 512], F32)) for i in range(8)]
        pqk = bank[0][:, :].rearrange("p (a n) -> p a n", a=2)
        pv = bank[1][:, 0:S].rearrange("p (t n) -> p t n", t=2)
        pkT = bank[2][:, 0:S].rearrange("p (t n) -> p t n", t=2)
        pnum = bank[3][:, :].rearrange("p (t n) -> p t n", t=2)
        poT = bank[4][:, 0:S]
        py = bank[5][:, 0:S].rearrange("p (t n) -> p t n", t=2)
        pkk = bank[6][:, 0:D + HEADS]
        px1T = [bank[1][:, S:2 * S], bank[2][:, S:2 * S]]
        pc = bank[7][:, 0:P].rearrange("p (t b c) -> p t b c", t=2, b=B)
        pkc = bank[0][:, 0:P].rearrange("p (t b c) -> p t b c", t=2, b=B)
        pkf = bank[0][:, P:2 * P].rearrange("p (a n) -> p a n", a=2)
        pqf = bank[1][:, 0:P].rearrange("p (a n) -> p a n", a=2)
        pcorr = bank[3][:, 0:S]
        prT = bank[4][:, 0:P].rearrange("p (h n) -> p h n", h=2)
        pO = [bank[6][:, :].rearrange("p (b n) -> p b n", b=4), bank[7][:, :].rearrange("p (b n) -> p b n", b=4)]
        plg = bank[2][:, 0:H * E].rearrange("p (t e) -> p t e", e=E)
        ppos = bank[2][:, P:P + H * E].rearrange("p (t e) -> p t e", e=E)
        pT = bank[5]
        pT2 = [bank[5], bank[1], bank[5], bank[5]]
        pH = [bank[0], bank[1], bank[3], bank[4]]
        pY = [bank[6][:, :].rearrange("p (t n) -> p t n", n=D), bank[7][:, :].rearrange("p (t n) -> p t n", n=D)]

        ld_w = sem("ld_w")
        ld_w2 = sem("ld_w2")
        ld_vec = sem("ld_vec")
        ld_tab = sem("ld_tab")
        ld_xT = [sem(f"ld_xT{i}") for i in range(4)]
        ld_x = sem("ld_x")
        ld_ctx = sem("ld_ctx")
        ld_dft = sem("ld_dft")
        ld_w1 = sem("ld_w1")
        ld_moe = sem("ld_moe")
        W1_high = sem("W1_high")
        W1_split = sem("W1_split")
        x2T_high = sem("x2T_high")
        x2T_split = sem("x2T_split")
        xeT_split = sem("xeT_split")
        slots_zeroed = sem("slots_zeroed")
        sums_begun = sem("sums_begun")
        consts_set = sem("consts_set")
        xe_set = sem("xe_set")
        ones_set = sem("ones_set")
        xbias = sem("xbias")
        dve_o = sem("dve_o")
        pool_o = sem("pool_o")
        qk_raw = sem("qk_raw")
        qk_parts = sem("qk_parts")
        qk_phi = sem("qk_phi")
        v_raw = sem("v_raw")
        v_biased = sem("v_biased")
        kT_raw = sem("kT_raw")
        kT_copied = sem("kT_copied")
        kk_raw = sem("kk_raw")
        kk_masked = sem("kk_masked")
        num_raw = sem("num_raw")
        o_ready = sem("o_ready")
        oT_raw = sem("oT_raw")
        oT_copied = sem("oT_copied")
        y_raw = sem("y_raw")
        y_summed = sem("y_summed")
        norm1_ready = sem("norm1_ready")
        x1_dve = sem("x1_dve")
        x1_pool = sem("x1_pool")
        x1_biased = sem("x1_biased")
        x1T_raw = sem("x1T_raw")
        x1T_copied = sem("x1T_copied")
        kc_raw = sem("kc_raw")
        kc_ready = sem("kc_ready")
        kf_raw = sem("kf_raw")
        kf_ready = sem("kf_ready")
        qc_raw = sem("qc_raw")
        qc_ready = sem("qc_ready")
        qf_raw = sem("qf_raw")
        spec_ready = sem("spec_ready")
        corr_raw = sem("corr_raw")
        top_ready = sem("top_ready")
        c_exp = sem("c_exp")
        xf_ready = sem("xf_ready")
        rT_raw = sem("rT_raw")
        rT_copied = sem("rT_copied")
        O_raw = sem("O_raw")
        norm2_ready = sem("norm2_ready")
        x2_dve = sem("x2_dve")
        x2_act = sem("x2_act")
        x2T_raw = sem("x2T_raw")
        x2T_copied = sem("x2T_copied")
        lg_raw = sem("lg_raw")
        pair_ready = sem("pair_ready")
        pos_raw = sem("pos_raw")
        diff_ready = sem("diff_ready")
        o2_summed = sem("o2_summed")
        lg_copied = sem("lg_copied")
        pos_copied = sem("pos_copied")
        gate_tanh = sem("gate_tanh")
        gates_ready = sem("gates_ready")
        slots_ready = sem("slots_ready")
        idx_ready = sem("idx_ready")
        scattered = sem("scattered")
        ld_slots = [sem(f"ld_slots{e}") for e in range(SPARSE)]
        added = [sem(f"added{i}") for i in range(2)]
        xeT_raw = sem("xeT_raw")
        xeT_high = sem("xeT_high")
        h_raw = sem("h_raw")
        h_gelu = sem("h_gelu")
        h_ready = sem("h_ready")
        ye_raw = sem("ye_raw")
        ye_taken = sem("ye_taken")
        ld_sum0 = [sem(f"ld_sum0_{h}") for h in range(2)]
        ld_sum1 = [sem(f"ld_sum1_{g}") for g in range(4)]
        summed_dve = sem("summed_dve")
        summed_pool = sem("summed_pool")
        norm3_ready = sem("norm3_ready")
        out_dve = sem("out_dve")
        out_act = sem("out_act")
        out_stored = sem("out_stored")

        dense, sparse = units()
        every = dense + sparse
        DLAG = 2

        def sparse_unit(u):
            return u - len(dense)

        block = ctx.enter_context(nc.Block())

        @block.sync
        def _(sp):
            sp.dma_start(xT[:, 0:512], xt[:, 0:512]).then_inc(ld_xT[0], 16)
            sp.dma_start(W[:, 0:W_O], weights[:, 0:W_O]).then_inc(ld_w, 16)
            sp.dma_start(vec[:, :], vectors.partition_broadcast(P)).then_inc(ld_vec, 16)
            sp.dma_start(tab[:, :], tables).then_inc(ld_tab, 16)
            sp.dma_start(x[:, :, :], xr.rearrange("(t p) d -> p t d", p=P)).then_inc(ld_x, 16)
            for i in range(1, 4):
                sp.dma_start(xT[:, 512 * i:512 * (i + 1)], xt[:, 512 * i:512 * (i + 1)]).then_inc(ld_xT[i], 16)
            sp.dma_start(W[:, W_O:], weights[:, W_O:]).then_inc(ld_w2, 16)
            sp.dma_start(ctxT[:, :], ctxt).then_inc(ld_ctx, 16)
            sp.dma_start(fwd[:, :, :], dft).then_inc(ld_dft, 16)
            sp.dma_start(inv[:, :, :], idft).then_inc(ld_dft, 16)
            sp.dma_start(W1[:, :, :], w1.rearrange("e d f -> d e f")).then_inc(ld_w1, 16)
            sp.dma_start(W2[:, :, :, :], w2.rearrange("e (c f) d -> f e c d", f=P)).then_inc(ld_moe, 16)
            sp.wait_ge(xe_set, 1)
            sp.dma_start(slots_d.rearrange("(p n) d -> p (n d)", p=P),
                         xe[:, :, :, :].rearrange("p s b d -> p (s b d)")).then_inc(slots_zeroed, 16)
            sp.dma_start(sum_d[1].rearrange("(p n) d -> p (n d)", p=P),
                         xe[:, :, :, :].rearrange("p s b d -> p (s b d)")[:, 0:NT * D]).then_inc(sums_begun, 16)

            def begin_sum(g):
                sp.wait_ge(ye_taken, DENSE * (g + 1))
                sp.dma_start(sum_d[0][512 * g:512 * (g + 1), :].rearrange("(t p) d -> p t d", p=P),
                             dacc[:, 4 * g:4 * g + 4, :]).then_inc(sums_begun, 16)

            begin_sum(0)
            begin_sum(1)
            sp.wait_ge(scattered, 16 * 2 * NT)
            for s in range(SPARSE):
                sp.dma_start(xe[:, s, :, :], slots_d[CAP * s:CAP * (s + 1), :].rearrange("(b p) d -> p b d", p=P)
                             ).then_inc(ld_slots[s], 16)
            begin_sum(2)
            begin_sum(3)
            sp.wait_ge(added[0], 16 * NBLK * SPARSE // 2)
            def load_sum0(h):
                sp.dma_start(sum0[:, H * h:H * (h + 1), :],
                             sum_d[0][N // 2 * h:N // 2 * (h + 1), :].rearrange("(t p) d -> p t d", p=P)
                             ).then_inc(ld_sum0[h], 16)

            load_sum0(0)
            sp.wait_ge(added[1], 16 * NBLK * SPARSE // 2)
            for g in range(4):
                sp.dma_start(sum1[:, 4 * g:4 * g + 4, :],
                             sum_d[1][512 * g:512 * (g + 1), :].rearrange("(t p) d -> p t d", p=P)).then_inc(ld_sum1[g], 16)
                if g == 1:
                    load_sum0(1)
            for g in range(4):
                sp.wait_ge(out_dve, g + 1)
                sp.wait_ge(out_act, g + 1)
                sp.dma_start(out[512 * g:512 * (g + 1), :].rearrange("(t p) d -> p t d", p=P),
                             res[:, 4 * g:4 * g + 4, :]).then_inc(out_stored, 16)
            sp.wait_ge(out_stored, 64)

        @block.tensor
        def _(pe):
            def keep_warm(n, into=bank[6]):
                for _ in range(n):
                    nc.tensor.matmul(into[:, :].rearrange("p (a n) -> p a n", a=4), ones16[:, :], ones16[:, :].unsqueeze(1).broadcast_to([P, 4, P]),
                                     start=True, stop=True)

            def project_qk(b):
                pe.wait_ge(ld_xT[b // 2], 16)
                if b >= 1:
                    pe.wait_ge(qk_parts, 4 * b)
                for a, w in ((0, W_Q), (1, W_K)):
                    last = nc.tensor.matmul(pqk[:, a, :], W[:, w:w + D], xT[:, S * b:S * (b + 1)], start=True, stop=True)
                last.then_inc(qk_raw, 1)

            def project_v(b):
                if b >= 1:
                    pe.wait_ge(v_biased, b)
                for t in range(2):
                    j = 2 * b + t
                    last = nc.tensor.matmul(pv[:, t, :], xT[:, P * j:P * (j + 1)], W[:, W_V:W_V + D],
                                            start=True, stop=True)
                last.then_inc(v_raw, 1)

            def turn_k(b):
                pe.wait_ge(qk_phi, b + 1)
                if b == 0:
                    pe.wait_ge(ld_tab, 16)
                if b >= 1:
                    pe.wait_ge(kT_copied, b)
                for t in range(2):
                    last = nc.tensor.transpose(pkT[:, t, :], phi[:, b % 2, 1, P * t:P * (t + 1)], ident)
                last.then_inc(kT_raw, 1)

            def keys_values(b):
                pe.wait_ge(kT_copied, b + 1)
                pe.wait_ge(v_biased, b + 1)
                if b == 0:
                    pe.wait_ge(ones_set, 1)
                if b >= 1:
                    pe.wait_ge(kk_masked, b)
                for t in range(2):
                    last = nc.tensor.matmul(pkk, kphi[:, b % 2, t, :], v[:, b % 2, t, :],
                                            start=(t == 0), stop=(t == 1))
                last.then_inc(kk_raw, 1)

            def attend(b):
                pe.wait_ge(kk_masked, b + 1)
                if b >= 1:
                    pe.wait_ge(o_ready, b)
                for t in range(2):
                    last = nc.tensor.matmul(pnum[:, t, 0:D + HEADS], phi[:, b % 2, 0, P * t:P * (t + 1)],
                                            kvm[:, b % 2, :], start=True, stop=True)
                last.then_inc(num_raw, 1)

            def turn_o(b):
                pe.wait_ge(o_ready, b + 1)
                if b >= 1:
                    pe.wait_ge(oT_copied, b)
                for t in range(2):
                    last = nc.tensor.transpose(poT[:, P * t:P * (t + 1)], o[:, b % 2, t, :], ident)
                last.then_inc(oT_raw, 1)

            def project_o(b):
                pe.wait_ge(oT_copied, b + 1)
                if b == 0:
                    pe.wait_ge(ld_w2, 16)
                if b >= 1:
                    pe.wait_ge(y_summed, b)
                for t in range(2):
                    last = nc.tensor.matmul(py[:, t, :], oT[:, b % 2, P * t:P * (t + 1)], W[:, W_O:W_O + D],
                                            start=True, stop=True)
                last.then_inc(y_raw, 1)

            def project_ctx(b):
                if b == 0:
                    pe.wait_ge(ld_ctx, 16)
                    pe.wait_ge(qk_parts, 4 * B)
                for t in range(2):
                    j = 2 * b + t
                    last = nc.tensor.matmul(pkc[:, t, b, :], ctxT[:, P * j:P * (j + 1)], W[:, W_XQ:W_XQ + XC],
                                            start=True, stop=True)
                last.then_inc(kc_raw, 1)

            def spectrum(into, of):
                for a in range(2):
                    for t in range(2):
                        last = nc.tensor.matmul(into[:, a, :], fwd[:, t, P * a:P * (a + 1)], of[:, t, :],
                                                start=(t == 0), stop=(t == 1))
                return last

            def turn_x1(b):
                pe.wait_ge(x1_dve, b // 2 + 1)
                if b % 2 and NORM1_DVE[b // 2] < 4:
                    pe.wait_ge(x1_pool, b // 2 + 1)
                if b >= 2:
                    pe.wait_ge(x1T_copied, b - 1)
                pe.wait_ge(kT_copied if b % 2 else v_biased, B)
                for t in range(2):
                    last = nc.tensor.transpose(px1T[b % 2][:, P * t:P * (t + 1)], x1[:, 2 * b + t, :], ident)
                last.then_inc(x1T_raw, 1)

            def project_x1(b):
                pe.wait_ge(x1T_copied, b + 1)
                for t in range(2):
                    last = nc.tensor.matmul(pc[:, t, b, :], x1T[:, b % 4, P * t:P * (t + 1)], W[:, W_XQ:W_XQ + XC],
                                            start=True, stop=True)
                last.then_inc(qc_raw, 1)

            pe.wait_ge(ld_w, 16)
            for i in range(ROUNDS):
                if i < B:
                    project_qk(i)
                if 2 <= i <= B + 1:
                    attend(i - 2)
                if i < B:
                    project_v(i)
                if 1 <= i <= B:
                    turn_k(i - 1)
                if 3 <= i <= B + 2:
                    project_o(i - 3)
                if 1 <= i <= B:
                    keys_values(i - 1)
                if 2 <= i <= B + 1:
                    turn_o(i - 2)
                for b in range(B):
                    if ROUND_CTX[b] == i:
                        project_ctx(b)
                if 9 <= i <= 12:
                    if i == 9:
                        pe.wait_ge(kk_masked, B)
                        pe.wait_ge(consts_set, 2)
                    keep_warm(2)
                if i == 12:
                    pe.wait_ge(kc_ready, 1)
                    pe.wait_ge(ld_dft, 32)
                    spectrum(pkf, kc).then_inc(kf_raw, 1)
                for b in range(B):
                    if ROUND_X1[b] == i:
                        if b >= 2:
                            project_x1(b - 2)
                        turn_x1(b)
            project_x1(B - 2)
            project_x1(B - 1)

            pe.wait_ge(qc_ready, 1)
            spectrum(pqf, qc).then_inc(qf_raw, 1)
            keep_warm(3)
            pe.wait_ge(spec_ready, 1)
            nc.tensor.matmul(pcorr, s1[:, 0:1].broadcast_to([P, P]), inv[:, 0, :], start=True, stop=False)
            pe.wait_ge(spec_ready, 2)
            nc.tensor.matmul(pcorr, s2[:, 0:1].broadcast_to([P, P]), inv[:, 1, :], start=False, stop=True).then_inc(corr_raw, 1)
            keep_warm(18)
            pe.wait_ge(xf_ready, 1)
            for h in range(2):
                for a in range(2):
                    last = nc.tensor.matmul(prT[:, h, :], inv[:, a, P * h:P * (h + 1)], xf[:, a, :],
                                            start=(a == 0), stop=(a == 1))
            last.then_inc(rT_raw, 1)
            keep_warm(4)
            for b in range(B):
                if b % 4 == 0:
                    pe.wait_ge(rT_copied, b // 4 + 1)
                last = nc.tensor.matmul(pO[b // 4][:, b % 4, :], rTw[:, b, :, :].rearrange("p n k -> p (n k)"),
                                        W[:, W_XO:W_XO + D], start=True, stop=True)
                if b % 4 == 3:
                    last.then_inc(O_raw, 1)

            def turn_x2(i, g):
                if NORM2_DVE[g]:
                    pe.wait_ge(x2_dve, sum(n > 0 for n in NORM2_DVE[:g + 1]))
                pe.wait_ge(x2_act, g + 1)
                if i >= 2:
                    pe.wait_ge(x2T_copied, i)
                for t in range(4):
                    last = nc.tensor.transpose(pT2[i][:, P * t:P * (t + 1)], x2g[:, 4 * i + t, 0:D], ident)
                last.then_inc(x2T_raw, 1)

            def logits(g):
                t0, n = GROUPS[g]
                pe.wait_ge(x2T_copied, (t0 + n) // 4)
                if g >= 1:
                    pe.wait_ge(pos_copied, g)
                for t in range(n):
                    j = t0 + t
                    last = nc.tensor.matmul(plg[:, t, :], x2T[:, P * j:P * (j + 1)], W[:, W_G:W_G + E],
                                            start=True, stop=True)
                last.then_inc(lg_raw, 1)

            def up(u):
                e, t0, n = every[u]
                if u == 0:
                    pe.wait_ge(x2T_copied, 2)
                pe.wait_ge(W1_split, e + 1)
                if u < len(dense):
                    pe.wait_ge(x2T_split, t0 // 4 + 1)
                    xh, xl = x2Th[:, t0 // 4 % 2, :], x2Tl[:, t0 // 4 % 2, :]
                else:
                    pe.wait_ge(xeT_split, sparse_unit(u) + 1)
                    xh, xl = xeTh[:, u % 2, 0:P * n], xeTl[:, u % 2, 0:P * n]
                for f, h in enumerate((0, 2, 1, 3)):
                    if u >= 1:
                        pe.wait_ge(h_gelu if h < 2 else h_ready, 2 * u - 1 + h % 2)
                    wh, wl = W1h[:, e, P * h:P * (h + 1)], W1l[:, e, P * h:P * (h + 1)]
                    nc.tensor.matmul(pH[h][:, 0:P * n], wh, xh, start=True, stop=False)
                    nc.tensor.matmul(pH[h][:, 0:P * n], wh, xl, start=False, stop=False)
                    nc.tensor.matmul(pH[h][:, 0:P * n], wl, xh, start=False, stop=True).then_inc(h_raw, 1)

            def down(u):
                e, t0, n = every[u]
                if u == 0:
                    pe.wait_ge(ld_moe, 16)
                pe.wait_ge(h_ready, 2 * (u + 1))
                if u >= 2:
                    pe.wait_ge(ye_taken, u - 1)
                if u < 2:
                    pe.wait_ge(o2_summed, 4 * (u + 1))
                for t in range(n):
                    for c in range(2):
                        last = nc.tensor.matmul(pY[u % 2][:, t, :], hT[:, u % NH, c, P * t:P * (t + 1)], W2[:, e, c, :],
                                                start=(c == 0), stop=(c == 1))
                last.then_inc(ye_raw, 1)

            def turn_xe(u):
                s = sparse_unit(u)
                e, b0, n = every[u]
                pe.wait_ge(ld_slots[e - DENSE], 16)
                if s >= 1:
                    pe.wait_ge(xeT_split, s)
                for t in range(n):
                    last = nc.tensor.transpose(pT[:, P * t:P * (t + 1)], xe[:, e - DENSE, b0 + t, 0:D], ident)
                last.then_inc(xeT_raw, 1)

            def places(g):
                pe.wait_ge(pair_ready, g + 1)
                pe.wait_ge(lg_copied, g + 1)
                if g == 0:
                    pe.wait_ge(consts_set, 2)
                t0, n = GROUPS[g]
                for i in range(t0):
                    nc.tensor.matmul(ppos[:, 0:n, :], ones16[:, :], m16[:, i:i + 1, :].broadcast_to([P, n, E]),
                                     start=(i == 0), stop=False, skip_group_check=True)
                nc.tensor.matmul(ppos[:, 0:n, :], tri16[:, :], m16[:, t0:t0 + n, :], start=(g == 0), stop=False,
                                 skip_group_check=True)
                for i in range(n - 1):
                    last = nc.tensor.matmul(ppos[:, i + 1:n, :], ones16[:, :],
                                            m16[:, t0 + i:t0 + i + 1, :].broadcast_to([P, n - 1 - i, E]),
                                            start=False, stop=(i == n - 2), skip_group_check=True)
                last.then_inc(pos_raw, 1)

            keep_warm(16, bank[0])
            turn_x2(0, 0)
            keep_warm(4, bank[0])
            logits(0)
            keep_warm(9, bank[0])
            turn_x2(1, 1)
            keep_warm(3, bank[0])
            places(0)
            for u in range(len(dense)):
                up(u)
                if u == 0:
                    logits(1)
                if u == 1:
                    turn_x2(2, 2)
                    places(1)
                    turn_x2(3, 2)
                if u == 2:
                    logits(2)
                if u >= DLAG:
                    down(u - DLAG)
                if u == 2:
                    places(2)
            n = len(dense)
            down(n - 2)
            turn_xe(n)
            down(n - 1)
            for u in range(n, len(every)):
                if u + 1 < len(every):
                    turn_xe(u + 1)
                up(u)
                if u > n:
                    down(u - 1)
            down(len(every) - 1)

        @block.scalar
        def _(act):
            def qk_part(b, a):
                act.wait_ge(qk_raw, b + 1)
                if b >= 2:
                    act.wait_ge(qk_phi, b - 1)
                bias = W[:, W_BQ + a:W_BQ + a + 1]
                nc.scalar.activation(qke[:, b % 2, a, :], pqk[:, a, :], ACT.Exp, bias=bias).then_inc(qk_parts, 1)
                nc.scalar.activation(qkr[:, b % 2, a, :], pqk[:, a, :], ACT.Relu, bias=bias).then_inc(qk_parts, 1)

            def copy_kT(b):
                act.wait_ge(kT_raw, b + 1)
                if b >= 2:
                    act.wait_ge(kk_raw, b - 1)
                nc.scalar.activation(kphi[:, b % 2, :, :], pkT, ACT.Copy).then_inc(kT_copied, 1)

            def copy_oT(b):
                act.wait_ge(oT_raw, b + 1)
                if b >= 2:
                    act.wait_ge(y_raw, b - 1)
                nc.scalar.activation(oT[:, b % 2, :], poT, ACT.Copy).then_inc(oT_copied, 1)

            def copy_x1T(b):
                act.wait_ge(x1T_raw, b + 1)
                if b >= 4:
                    act.wait_ge(qc_raw, b - 3)
                nc.scalar.activation(x1T[:, b % 4, :], px1T[b % 2], ACT.Copy).then_inc(x1T_copied, 1)

            act.wait_ge(ld_w, 16)
            for i in range(ROUNDS):
                if i < B:
                    qk_part(i, 0)
                if 1 <= i <= B:
                    copy_kT(i - 1)
                if i < B:
                    qk_part(i, 1)
                if 2 <= i <= B + 1:
                    copy_oT(i - 2)
                if 7 <= i <= 10:
                    if i == 7:
                        act.wait_ge(ld_w1, 16)
                    for e in (2 * i - 14, 2 * i - 13):
                        nc.scalar.activation(W1h[:, e, :], W1[:, e, :], ACT.Copy).then_inc(W1_high, 1)
                for b in range(B):
                    if ROUND_X1[b] == i:
                        copy_x1T(b)
            act.wait_ge(top_ready, 1)
            nc.scalar.activation(cexp[:, :], pcorr, ACT.Exp, bias=ntop[:, 0:1]).then_inc(c_exp, 1)

            def norm(to, tiles, count, n, done):
                act.wait_ge(count, n)
                for t in tiles:
                    last = nc.scalar.activation(to(t), r[:, t, :], ACT.Identity, scale=rs[:, t:t + 1], bias=nmr[:, t:t + 1])
                last.then_inc(done, 1)

            def copy_x2T(i):
                act.wait_ge(x2T_raw, i + 1)
                nc.scalar.activation(x2T[:, 512 * i:512 * (i + 1)], pT2[i][:, :], ACT.Copy).then_inc(x2T_copied, 1)

            def high_x2T(i):
                act.wait_ge(x2T_copied, i + 1)
                if i >= 2:
                    act.wait_ge(h_raw, 4 * DENSE * (i - 1))
                nc.scalar.activation(x2Th[:, i % 2, :], x2T[:, 512 * i:512 * (i + 1)], ACT.Copy).then_inc(x2T_high, 1)

            def norm2(g):
                t0, n = GROUPS[g]
                norm(lambda t: x2g[:, t, 0:D], range(t0 + NORM2_DVE[g], t0 + n), norm2_ready, g + 1, x2_act)

            def gates(g):
                act.wait_ge(diff_ready, g + 1)
                t0, n = GROUPS[g]
                nc.scalar.activation(th[:, t0:t0 + n], gd[:, t0:t0 + n], ACT.Tanh, scale=0.5).then_inc(gate_tanh, 1)

            def gelu(u):
                e, t0, n = every[u]
                for c in range(2):
                    act.wait_ge(h_raw, 4 * u + (1 if c == 0 else 3))
                    if u >= 1:
                        act.wait_ge(h_ready, 2 * u - 1 + c)
                    nc.scalar.activation(gel[:, c, 0:P * n], pH[c][:, 0:P * n], ACT.Gelu).then_inc(h_gelu, 1)

            def copy_xe(u):
                s = sparse_unit(u)
                e, b0, n = every[u]
                act.wait_ge(xeT_raw, s + 1)
                if s >= 2:
                    act.wait_ge(h_raw, 4 * (u - 1))
                nc.scalar.activation(xeTh[:, u % 2, 0:P * n], pT[:, 0:P * n], ACT.Copy).then_inc(xeT_high, 1)

            norm2(0)
            copy_x2T(0)
            high_x2T(0)
            norm2(1)
            copy_x2T(1)
            gates(0)
            high_x2T(1)
            gelu(0)
            norm2(2)
            gates(1)
            gelu(1)
            copy_x2T(2)
            copy_x2T(3)
            high_x2T(2)
            gelu(2)
            gates(2)
            gelu(3)
            high_x2T(3)
            for u in range(4, len(dense)):
                gelu(u)
            n = len(dense)
            copy_xe(n)
            for u in range(n, len(every)):
                if u + 1 < len(every):
                    copy_xe(u + 1)
                gelu(u)
            for g in range(4):
                norm(lambda t: res[:, t, :], range(4 * g + NORM3_DVE[g], 4 * g + 4), norm3_ready, g // 2 + 1, out_act)

        @block.gpsimd
        def _(pool):
            order = Order(pool, pool_o)
            nc.gpsimd.memset(v[:, :, :, D:], 1.0).then_inc(ones_set, 1)
            nc.gpsimd.memset(xe[:, :, :, :], 0.0).then_inc(xe_set, 1)
            nc.gpsimd.memset(ones16[:, :], 1.0).then_inc(consts_set, 1)
            pool.wait_ge(ld_tab, 16)
            order.done(nc.gpsimd.tensor_copy(x2g[:, :, D + E:].rearrange("p t o -> p (t o)"), tab[:, T_TOK:T_TOK + NT]))

            def bias_x(b):
                j = 2 * b
                nc.gpsimd.tensor_tensor(x[:, j:j + 2, :], x[:, j:j + 2, :],
                                        vec[:, V_O:V_O + D].unsqueeze(1).broadcast_to([P, 2, D]), ALU.add).then_inc(xbias, 1)

            def bias_x1(b):
                pool.wait_ge(x1T_raw, b + 1)
                j = 2 * b
                nc.gpsimd.tensor_tensor(x1[:, j:j + 2, :], x1[:, j:j + 2, :],
                                        vec[:, V_XO:V_XO + D].unsqueeze(1).broadcast_to([P, 2, D]), ALU.add).then_inc(x1_biased, 1)

            def norm1(g):
                pool.wait_ge(norm1_ready, g + 1)
                for t in range(4 * g + NORM1_DVE[g], 4 * g + 4):
                    ins = nc.gpsimd.tensor_scalar(x1[:, t, :], r[:, t, :], mv[:, t, 0:1], rs[:, t:t + 1],
                                                  ALU.subtract, ALU.mult)
                ins.then_inc(x1_pool, 1)

            pool.wait_ge(ld_x, 16)
            pool.wait_ge(ld_vec, 16)
            for b in range(B):
                bias_x(b)

            def split_w1(e):
                pool.wait_ge(W1_high, e + 1)
                nc.gpsimd.tensor_tensor(W1l[:, e, :], W1[:, e, :], W1h[:, e, :].bitcast(F32), ALU.subtract
                                        ).then_inc(W1_split, 1)

            norm1(0)
            split_w1(0)
            split_w1(1)
            norm1(1)
            split_w1(2)
            bias_x1(0)
            bias_x1(1)
            norm1(2)
            split_w1(3)
            for b in range(2, B):
                bias_x1(b)
            for e in range(4, E):
                split_w1(e)

            def scatter(g):
                pool.wait_ge(slots_ready, g + 1)
                pool.wait_ge(gates_ready, g + 1)
                if NORM2_DVE[g]:
                    pool.wait_ge(x2_dve, sum(n > 0 for n in NORM2_DVE[:g + 1]))
                pool.wait_ge(x2_act, g + 1)
                t0, n = GROUPS[g]
                for t in range(t0, t0 + n):
                    for k in range(2):
                        nc.gpsimd.indirect_dma_start(
                            slots_d[:, :], bass.IndirectOffsetOnAxis(ap=slot[:, t, k:k + 1], axis=0),
                            x2g[:, t, :], None, bounds_check=SPARSE * CAP - 1, oob_is_err=False
                        ).then_inc(scattered, 16)

            def add_rows(u):
                e, b0, n = every[u]
                s = e - DENSE
                pool.wait_ge(idx_ready, s + 1)
                pool.wait_ge(ye_taken, u + 1)
                if s >= 2 and b0 == 0:
                    pool.wait_ge(added[s % 2], 16 * NBLK * (s // 2))
                for b in range(b0, b0 + n):
                    nc.gpsimd.indirect_dma_start(
                        sum_d[s % 2][:, :], bass.IndirectOffsetOnAxis(ap=idx[:, s, b:b + 1], axis=0),
                        ye[s // 3][:, s % 3, b, :], None, bounds_check=N - 1, oob_is_err=False,
                        compute_op=ALU.add).then_inc(added[s % 2], 16)

            pool.wait_ge(slots_zeroed, 16)
            for g in range(len(GROUPS)):
                scatter(g)
            pool.wait_ge(sums_begun, 16 * 5)
            for u in range(len(dense), len(every)):
                add_rows(u)
            pool.wait_ge(ld_sum0[1], 16)
            for g in (2, 3):
                pool.wait_ge(ld_sum1[g], 16)
                nc.gpsimd.tensor_tensor(r[:, 4 * g:4 * g + 4, :], sum0[:, 4 * g:4 * g + 4, :],
                                        sum1[:, 4 * g:4 * g + 4, :], ALU.add).then_inc(summed_pool, 1)

        @block.vector
        def _(dve):
            order = Order(dve, dve_o)
            tt, ts, stt = nc.vector.tensor_tensor, nc.vector.tensor_scalar, nc.vector.scalar_tensor_tensor

            def bias_v(b):
                dve.wait_ge(v_raw, b + 1)
                if b >= 2:
                    dve.wait_ge(kk_raw, b - 1)
                tt(v[:, b % 2, :, 0:D], pv, vec[:, V_V:V_V + D].unsqueeze(1).broadcast_to([P, 2, D]),
                   ALU.add).then_inc(v_biased, 1)

            def phi_qk(b):
                dve.wait_ge(qk_parts, 4 * (b + 1))
                if b >= 2:
                    dve.wait_ge(kT_raw, b - 1)
                    dve.wait_ge(num_raw, b - 1)
                stt(phi[:, b % 2, :, :], qke[:, b % 2, :, :], 1.0, qkr[:, b % 2, :, :], ALU.min, ALU.add).then_inc(qk_phi, 1)

            def mask_kk(b):
                dve.wait_ge(kk_raw, b + 1)
                if b == 0:
                    dve.wait_ge(ld_tab, 16)
                if b >= 2:
                    dve.wait_ge(num_raw, b - 1)
                tt(kvm[:, b % 2, 0:D], pkk[:, 0:D], tab[:, T_HEAD:T_HEAD + D], ALU.mult)
                stt(kvm[:, b % 2, D:], pkk[:, D:], ATT_EPS, tab[:, T_HEAD + D:T_HEAD + D + HEADS],
                    ALU.add, ALU.mult).then_inc(kk_masked, 1)

            def normaliser(b):
                dve.wait_ge(num_raw, b + 1)
                return order.mark(ts(z0[:, :, :], pnum[:, :, D:D + HEADS], ATT_EPS, None, ALU.add))

            def normaliser_inverse(after):
                order.wait(after)
                return order.mark(nc.vector.reciprocal(z1[:, :, :], z0[:, :, :]))

            def normalise(b, after):
                if b >= 2:
                    dve.wait_ge(oT_raw, b - 1)
                order.wait(after)
                tt(o[:, b % 2, :, :].rearrange("p t (h c) -> p t h c", c=DK),
                   pnum[:, :, 0:D].rearrange("p t (h c) -> p t h c", c=DK),
                   z1[:, :, :].unsqueeze(3).broadcast_to([P, 2, HEADS, DK]), ALU.mult).then_inc(o_ready, 1)

            def residual1(b):
                dve.wait_ge(y_raw, b + 1)
                dve.wait_ge(xbias, b + 1)
                j = 2 * b
                tt(r[:, j:j + 2, :], py, x[:, j:j + 2, :], ALU.add).then_inc(y_summed, 1)

            def statistics(t0, t1, count, n):
                dve.wait_ge(count, n)
                for t in range(t0, t1):
                    last = nc.vector.bn_stats(stats[:, t, :], r[:, t, :])
                return order.mark(last)

            def moments(t0, t1, after):
                order.wait(after)
                for t in range(t0, t1):
                    last = nc.vector.bn_aggr(mv[:, t, :], stats[:, t, :])
                return order.mark(last)

            def rsqrt_step(k, t0, t1, after, done=None):
                v, h, y, a = var[:, t0:t1], half[:, t0:t1], rs[:, t0:t1], ra[:, t0:t1]
                order.wait(after)
                if k == 0:
                    ins = ts(v, mv[:, t0:t1, 1:2].rearrange("p t o -> p (t o)"), LN_EPS, None, ALU.add)
                elif k == 1:
                    ins = ts(h, v.bitcast(I32), 1, None, ALU.logical_shift_right)
                elif k == 2:
                    ins = ts(y.bitcast(I32), h, -1.0, RSQRT_SEED, ALU.mult, ALU.add)
                elif k == 3:
                    ins = stt(a, y, -RSQRT_A, y, ALU.mult, ALU.mult)
                elif k == 5:
                    ins = stt(y, a, RSQRT_B, y, ALU.add, ALU.mult)
                elif k == 6:
                    ins = stt(a, y, -0.5, y, ALU.mult, ALU.mult)
                elif k == 8:
                    ins = stt(y, a, 1.5000003, y, ALU.add, ALU.mult)
                else:
                    ins = tt(a, a, v, ALU.mult)
                if done:
                    ins.then_inc(done, 1)
                    return None
                return order.mark(ins)

            def shift(t0, t1, after):
                order.wait(after)
                return stt(nmr[:, t0:t1], mv[:, t0:t1, 0:1].rearrange("p t o -> p (t o)"), -1.0, rs[:, t0:t1],
                           ALU.mult, ALU.mult)

            def apply_norm(to, t):
                return ts(to(t), r[:, t, :], mv[:, t, 0:1], rs[:, t:t + 1], ALU.subtract, ALU.mult)

            def prepare_k():
                dve.wait_ge(kf_raw, 1)
                order.done(nc.vector.tensor_copy(kf[:, :, :], pkf))
                c = [tab[:, T_SCALE + i:T_SCALE + i + 1] for i in range(8)]
                ka, kb = kf[:, 0, :], kf[:, 1, :]
                ts(k1[:, 0, :], ka, c[0], None, ALU.mult)
                ts(k1[:, 1, :], kb, c[1], None, ALU.mult)
                ts(k2[:, 0, :], kb, c[2], None, ALU.mult)
                ts(k2[:, 1, :], ka, c[1], None, ALU.mult)
                ts(va[:, 0, :], ka, c[4], None, ALU.mult)
                ts(va[:, 1, :], kb, c[5], None, ALU.mult)
                ts(vb[:, 0, :], kb, c[5], None, ALU.mult)
                order.done(ts(vb[:, 1, :], ka, c[6], None, ALU.mult))
                stt(k2[:, 1, :], kb, c[3], k2[:, 1, :], ALU.mult, ALU.add)
                ins = stt(vb[:, 1, :], kb, c[7], vb[:, 1, :], ALU.mult, ALU.add)
                ins.then_inc(kf_ready, 1)

            dve.wait_ge(ld_vec, 16)
            stats_n, rs_n = 0, 0
            for i in range(ROUNDS - 1):
                begin = i >= 5 and i % 2 == 1
                end = i >= 6 and i % 2 == 0
                g0 = 4 * ((i - 5) // 2)

                def step(k):
                    return rsqrt_step(k, g0, g0 + 4, rs_n)

                if 2 <= i <= B + 1:
                    z_n = normaliser(i - 2)
                if end:
                    rs_n = step(4)
                if i < B:
                    bias_v(i)
                if end:
                    rs_n = step(5)
                if 2 <= i <= B + 1:
                    z_n = normaliser_inverse(z_n)
                if end:
                    rs_n = step(6)
                if 4 <= i <= B + 3:
                    rs_n2 = moments(2 * (i - 4), 2 * (i - 4) + 2, stats_n)
                if end:
                    rs_n = step(7)
                if 2 <= i <= B + 1:
                    normalise(i - 2, z_n)
                if begin:
                    rs_n = rsqrt_step(0, g0, g0 + 4, rs_n2)
                if 1 <= i <= B:
                    mask_kk(i - 1)
                if end:
                    rsqrt_step(8, g0, g0 + 4, rs_n, norm1_ready)
                if begin:
                    rs_n = step(1)
                if 3 <= i <= B + 2:
                    residual1(i - 3)
                if begin:
                    rs_n = step(2)
                if end:
                    dve.wait_ge(norm1_ready, g0 // 4 + 1)
                    for t in range(g0, g0 + NORM1_DVE[g0 // 4]):
                        last = apply_norm(lambda t: x1[:, t, :], t)
                    last.then_inc(x1_dve, 1)
                if i < B:
                    phi_qk(i)
                if 3 <= i <= B + 2:
                    stats_n = statistics(2 * (i - 3), 2 * (i - 3) + 2, y_summed, i - 2)
                if begin:
                    rs_n = step(3)
                if i == 1:
                    nc.vector.tensor_copy(tri16[:, :], tab[:, T_TRI:T_TRI + P]).then_inc(consts_set, 1)
                if i == 11:
                    dve.wait_ge(kc_raw, B)
                    tt(kc[:, :, :].rearrange("p t (b c) -> p t b c", c=XC), pkc,
                       vec[:, V_XQ:V_XQ + XC].unsqueeze(1).unsqueeze(1).broadcast_to([P, 2, B, XC]), ALU.add).then_inc(kc_ready, 1)

            prepare_k()
            dve.wait_ge(qc_raw, B)
            tt(qc[:, :, :].rearrange("p t (b c) -> p t b c", c=XC), pc,
               vec[:, V_XQ:V_XQ + XC].unsqueeze(1).unsqueeze(1).broadcast_to([P, 2, B, XC]), ALU.add).then_inc(qc_ready, 1)
            dve.wait_ge(qf_raw, 1)
            dve.wait_ge(kf_ready, 1)
            qf = pqf.rearrange("p a n -> p (a n)")
            nc.vector.tensor_tensor_reduce(
                out=junk[:, 0:P], in0=qf, in1=k1[:, :, :].rearrange("p a n -> p (a n)"), scale=1.0, scalar=0.0,
                op0=ALU.mult, op1=ALU.add, accum_out=s1[:, :]).then_inc(spec_ready, 1)
            nc.vector.tensor_tensor_reduce(
                out=junk2[:, 0:P], in0=qf, in1=k2[:, :, :].rearrange("p a n -> p (a n)"), scale=1.0, scalar=0.0,
                op0=ALU.mult, op1=ALU.add, accum_out=s2[:, :]).then_inc(spec_ready, 1)
            dve.wait_ge(corr_raw, 1)
            order.done(nc.vector.max(top1[:, :], pcorr))
            order.done(nc.vector.match_replace(corr1[:, :], top1[:, :], pcorr, LOW))
            ts(ntop[:, :], top1[:, 0:1], -1.0, None, ALU.mult).then_inc(top_ready, 1)
            order.done(nc.vector.max(top2[:, :], corr1[:, :]))
            order.done(nc.vector.memset(top2[:, TOPK - 8:], LOW))
            order.done(nc.vector.match_replace(corr2[:, :], top2[:, :], corr1[:, :], LOW))
            dve.wait_ge(c_exp, 1)
            order.done(stt(cw[:, :], corr2[:, :], LOW, cexp[:, :], ALU.is_equal, ALU.mult, accum_out=csum[:, :]))
            nc.vector.tensor_tensor_reduce(out=junk[:, :], in0=cw[:, :], in1=inv[:, 0, :], scale=1.0, scalar=0.0,
                                           op0=ALU.mult, op1=ALU.add, accum_out=wa[:, :])
            order.done(nc.vector.tensor_tensor_reduce(out=junk2[:, :], in0=cw[:, :], in1=inv[:, 1, :], scale=1.0, scalar=0.0,
                                                      op0=ALU.mult, op1=ALU.add, accum_out=wb[:, :]))
            order.done(ts(xf[:, :, :], va[:, :, :], wa[:, 0:1], None, ALU.mult))
            stt(xf[:, :, :], vb[:, :, :], wb[:, 0:1], xf[:, :, :], ALU.mult, ALU.add).then_inc(xf_ready, 1)
            order.done(nc.vector.reciprocal(crec[:, :], csum[:, :]))
            dve.wait_ge(rT_raw, 1)
            order.done(ts(rT[:, :, :].rearrange("p b (c h) -> p h b c", h=2),
                          prT.rearrange("p h (b c) -> p h b c", c=XC), crec[:, 0:1], None, ALU.mult))
            for b in (0, 4):
                nc.vector.tensor_copy(rTw[:, b:b + 4, :, :],
                                      rT[:, b:b + 4, :].unsqueeze(2).broadcast_to([P, 4, P // 16, 16])).then_inc(rT_copied, 1)
            def residual2(b):
                if b % 4 == 0:
                    dve.wait_ge(O_raw, b // 4 + 1)
                dve.wait_ge(x1_biased, b + 1)
                j = 2 * b
                tt(r[:, j:j + 2, :], x1[:, j:j + 2, :],
                   pO[b // 4][:, b % 4:b % 4 + 1, :].broadcast_to([P, 2, D]), ALU.add).then_inc(o2_summed, 1)

            def sum_piece(g, k):
                t0, n = GROUPS[g]
                if k < n // 2:
                    residual2(t0 // 2 + k)
                    return None
                t = t0 + k - n // 2
                dve.wait_ge(o2_summed, t // 2 + 1)
                return order.mark(nc.vector.bn_stats(stats[:, t, :], r[:, t, :]))

            def norm2(g, last):
                t0, n = GROUPS[g]
                more = GROUPS[g + 1][1] * 3 // 2 if g + 1 < len(GROUPS) else 0
                done = 0
                at = moments(t0, t0 + n, last)
                for k in range(RSQRT_OPS):
                    at = rsqrt_step(k, t0, t0 + n, at)
                    if done < more and k >= RSQRT_OPS - more:
                        last = sum_piece(g + 1, done)
                        done += 1
                shift(t0, t0 + n, at).then_inc(norm2_ready, 1)
                for t in range(t0, t0 + NORM2_DVE[g]):
                    ins = apply_norm(lambda t: x2g[:, t, 0:D], t)
                if NORM2_DVE[g]:
                    ins.then_inc(x2_dve, 1)
                return last, done

            def gating(u):
                e, t0, n = every[u]
                for c in range(2):
                    dve.wait_ge(h_gelu, 2 * u + 1 + c)
                    dve.wait_ge(h_raw, 4 * u + (2 if c == 0 else 4))
                    if u >= NH:
                        dve.wait_ge(ye_raw, u - NH + 1)
                    tt(hT[:, u % NH, c, 0:P * n], pH[2 + c][:, 0:P * n], gel[:, c, 0:P * n], ALU.mult).then_inc(h_ready, 1)

            def picks(g):
                t0, n = GROUPS[g]
                T = slice(t0, t0 + n)
                dve.wait_ge(lg_raw, g + 1)
                nc.vector.tensor_copy(lg[:, T, :], plg[:, 0:n, :]).then_inc(lg_copied, 1)
                dve.wait_ge(lg_copied, g + 1)
                for t in range(t0, t0 + n):
                    last = nc.vector.max(top[:, t, :], lg[:, t, :])
                order.done(last)
                tt(gd[:, T], top[:, T, 1:2].rearrange("p t o -> p (t o)"), top[:, T, 0:1].rearrange("p t o -> p (t o)"),
                   ALU.subtract).then_inc(diff_ready, 1)
                for t in range(t0, t0 + n):
                    last = nc.vector.max_index(topi[:, t, :], top[:, t, :], lg[:, t, :])
                order.done(last)
                order.done(nc.vector.tensor_copy(pick[:, T, :], topi[:, T, 0:2]))
                order.done(tt(oh[:, T, :, :].rearrange("p t k e -> p (t k) e"),
                              tab[:, T_EXP:T_EXP + E].unsqueeze(1).broadcast_to([P, 2 * n, E]),
                              pick[:, T, :].rearrange("p t k -> p (t k)").unsqueeze(2).broadcast_to([P, 2 * n, E]),
                              ALU.is_equal))
                tt(m16[:, T, :], oh[:, T, 0, :], oh[:, T, 1, :], ALU.add).then_inc(pair_ready, 1)
                tt(pair[:, T, :], oh[:, T, 0, :], oh[:, T, 1, :], ALU.add)
                order.done(tt(side[:, T, :], oh[:, T, 1, :], oh[:, T, 0, :], ALU.subtract))

            def slots_and_gates(g):
                t0, n = GROUPS[g]
                T = slice(t0, t0 + n)
                dve.wait_ge(gate_tanh, g + 1)
                g_n = order.mark(tt(gate[:, T, :], side[:, T, :], th[:, T].unsqueeze(2).broadcast_to([P, n, E]), ALU.mult))
                dve.wait_ge(pos_raw, g + 1)
                nc.vector.tensor_copy(place[:, T, :], ppos[:, 0:n, :]).then_inc(pos_copied, 1)
                order.wait(g_n)
                g_n = order.mark(tt(gate[:, T, :], gate[:, T, :], pair[:, T, :], ALU.add))
                dve.wait_ge(pos_copied, g + 1)
                s_n = order.mark(ts(over[:, T, :], place[:, T, :], float(CAP), float(FAR), ALU.is_ge, ALU.mult))
                tt(sv[:, T, :], place[:, T, :], tab[:, T_SLOT:T_SLOT + E].unsqueeze(1).broadcast_to([P, n, E]), ALU.add)
                keep_n = order.mark(ts(place[:, T, :], place[:, T, :], float(CAP), 0.5, ALU.is_lt, ALU.mult))
                order.wait(keep_n)
                s_n = order.mark(tt(sv[:, T, :], sv[:, T, :], over[:, T, :], ALU.add))
                tt(x2g[:, T, D:D + E], gate[:, T, :], place[:, T, :], ALU.mult).then_inc(gates_ready, 1)
                order.wait(s_n)
                for k in range(2):
                    ins = tt(ohs[:, T, k, :], oh[:, T, k, :], sv[:, T, :], ALU.mult)
                order.done(ins)
                order.done(nc.vector.tensor_reduce(slot_f[:, T, :].rearrange("p t k -> p (t k)"),
                                                   ohs[:, T, :, :].rearrange("p t k e -> p (t k) e"), AX.X, ALU.add))
                nc.vector.tensor_copy(slot[:, T, :], slot_f[:, T, :]).then_inc(slots_ready, 1)

            def split_x2T(i):
                dve.wait_ge(x2T_high, i + 1)
                if i >= 2:
                    dve.wait_ge(h_raw, 4 * DENSE * (i - 1))
                tt(x2Tl[:, i % 2, :], x2T[:, 512 * i:512 * (i + 1)], x2Th[:, i % 2, :].bitcast(F32), ALU.subtract
                   ).then_inc(x2T_split, 1)

            def split_xeT(u):
                e, b0, n = every[u]
                s = sparse_unit(u)
                dve.wait_ge(xeT_high, s + 1)
                if s >= 2:
                    dve.wait_ge(h_raw, 4 * (u - 1))
                tt(xeTl[:, u % 2, 0:P * n], pT[:, 0:P * n], xeTh[:, u % 2, 0:P * n].bitcast(F32), ALU.subtract
                   ).then_inc(xeT_split, 1)

            def take_dense(u):
                e, t0, n = every[u]
                dve.wait_ge(ye_raw, u + 1)
                dve.wait_ge(gates_ready, min(len(GROUPS), 1 + t0 // 4))
                if u >= 1:
                    dve.wait_ge(ye_taken, u)
                for t in range(n):
                    j = t0 + t
                    base = x2g[:, j, 0:D] if e == 0 else dacc[:, j, :]
                    last = stt(dacc[:, j, :], pY[u % 2][:, t, :], x2g[:, j, D + e:D + e + 1], base, ALU.mult, ALU.add)
                last.then_inc(ye_taken, 1)

            def take_sparse(u):
                e, b0, n = every[u]
                s = e - DENSE
                if b0 == 0:
                    dve.wait_ge(ld_slots[s], 16)
                    ts(idx[:, s, :], xe[:, s, :, D + E:].rearrange("p b o -> p (b o)"), float(FAR), None, ALU.add
                       ).then_inc(idx_ready, 1)
                dve.wait_ge(ye_raw, u + 1)
                tt(ye[s // 3][:, s % 3, b0:b0 + n, :], pY[u % 2][:, 0:n, :],
                   xe[:, s, b0:b0 + n, D + e:D + e + 1].broadcast_to([P, n, D]), ALU.mult).then_inc(ye_taken, 1)

            for k in range(6):
                last = sum_piece(0, k)
            last, _ = norm2(0, last)
            last, done = norm2(1, last)
            picks(0)
            split_x2T(0)
            slots_and_gates(0)
            for k in range(done, GROUPS[2][1] * 3 // 2):
                last = sum_piece(2, k)
            norm2(2, last)
            gating(0)
            picks(1)
            split_x2T(1)
            gating(1)
            slots_and_gates(1)
            gating(2)
            split_x2T(2)
            picks(2)
            slots_and_gates(2)
            take_dense(0)
            gating(3)
            for u in range(4, len(dense)):
                take_dense(u - 3)
                gating(u)
                if u == 4:
                    split_x2T(3)
            take_dense(len(dense) - 3)
            n = len(dense)
            take_dense(n - 2)
            split_xeT(n)
            take_dense(n - 1)
            for u in range(n, len(every)):
                if u + 1 < len(every):
                    split_xeT(u + 1)
                gating(u)
                if u > n:
                    take_sparse(u - 1)
            take_sparse(len(every) - 1)
            def norm3(g):
                for t in range(4 * g, 4 * g + NORM3_DVE[g]):
                    ins = apply_norm(lambda t: res[:, t, :], t)
                ins.then_inc(out_dve, 1)

            def bn3(t):
                dve.wait_ge(summed_dve if t < H else summed_pool, t % H // 4 + 1)
                return order.mark(nc.vector.bn_stats(stats[:, t, :], r[:, t, :]))

            dve.wait_ge(ld_sum0[0], 16)
            for g in range(2):
                dve.wait_ge(ld_sum1[g], 16)
                tt(r[:, 4 * g:4 * g + 4, :], sum0[:, 4 * g:4 * g + 4, :], sum1[:, 4 * g:4 * g + 4, :], ALU.add
                   ).then_inc(summed_dve, 1)
            for t in range(H):
                last = bn3(t)
            n = moments(0, H, last)
            for k in range(RSQRT_OPS):
                n = rsqrt_step(k, 0, H, n)
                if k < H:
                    last = bn3(H + k)
            shift(0, H, n).then_inc(norm3_ready, 1)
            n = moments(H, NT, last)
            for k in range(RSQRT_OPS):
                n = rsqrt_step(k, H, NT, n)
                if k < 2:
                    norm3(k)
            shift(H, NT, n).then_inc(norm3_ready, 1)
            norm3(2)
            norm3(3)


def kernel(x, ctx_1024, L0_attn_Wq, L0_attn_bq, L0_attn_Wk, L0_attn_bk, L0_attn_Wv, L0_attn_bv, L0_attn_Wo,
           L0_attn_bo, L0_xattn_Wq, L0_xattn_bq, L0_xattn_Wout, L0_xattn_bout, L0_ffn_Wg, L0_ffn_W1, L0_ffn_W2):
    import numpy as np
    import concourse.bacc as bacc
    from concourse.bass_utils import run_bass_kernel_spmd

    a = np.asarray
    xr = np.ascontiguousarray(a(x).reshape(N, D))
    weights = np.concatenate([a(L0_attn_Wq).T, a(L0_attn_Wk).T, a(L0_attn_bq).reshape(D, 1),
                              a(L0_attn_bk).reshape(D, 1), a(L0_attn_Wv).T,
                              a(L0_attn_Wo).T, a(L0_xattn_Wq), a(L0_xattn_Wout), a(L0_ffn_Wg).T], axis=1)
    vectors = np.concatenate([a(L0_attn_bv), a(L0_attn_bo), a(L0_xattn_bq), a(L0_xattn_bout)])

    p = np.arange(P)[:, None]
    tab = np.zeros((P, T_END), np.float32)
    tab[:, T_ID:T_ID + P] = np.eye(P)
    tab[:, T_HEAD:T_HEAD + D] = p // DK == np.arange(D)[None] // DK
    tab[:, T_HEAD + D:T_HEAD + D + HEADS] = p // DK == np.arange(HEADS)[None]
    scale = np.where(p[:, 0] == 0, 1.0, 2.0) / S
    rest = np.where(p[:, 0] == 0, 0.0, 1.0)
    mean = 1.0 / (B * XC)
    for i, c in enumerate([scale * mean, scale * rest * mean, -scale * rest * mean, scale * (1 - rest) * mean,
                           scale, scale * rest, -scale * rest, scale * (1 - rest)]):
        tab[:, T_SCALE + i] = c
    tab[:, T_EXP:T_EXP + E] = np.arange(E)
    tab[:, T_SLOT:T_SLOT + E] = np.where(np.arange(E) < DENSE, FAR, CAP * (np.arange(E) - DENSE))
    tab[:, T_TOK:T_TOK + NT] = p + P * np.arange(NT)[None] - FAR
    tab[:, T_TRI:T_TRI + P] = p < np.arange(P)[None]
    time, turn = np.arange(S)[:, None], np.arange(P)[None]
    angle = 2 * np.pi * ((time * turn) % S) / S
    basis = np.concatenate([np.cos(angle), np.sin(angle)], axis=1)
    basis[:, P] = 1 - 2 * (np.arange(S) % 2)
    dft = basis.reshape(2, P, S).transpose(1, 0, 2)
    idft = basis.T.reshape(2, P, S).transpose(1, 0, 2)

    arrays = {
        "xt": np.ascontiguousarray(xr.T), "xr": xr, "ctxt": np.ascontiguousarray(a(ctx_1024).reshape(N, D).T),
        "weights": np.ascontiguousarray(weights), "vectors": vectors, "tables": tab,
        "dft": np.ascontiguousarray(dft.astype(np.float32)), "idft": np.ascontiguousarray(idft.astype(np.float32)),
        "w1": np.ascontiguousarray(a(L0_ffn_W1)), "w2": np.ascontiguousarray(a(L0_ffn_W2)),
    }
    nc = bacc.Bacc("TRN2", target_bir_lowering=False, num_devices=1)
    args = [nc.dram_tensor(f"in_{name}", v.shape, mybir.dt.from_np(v.dtype), kind="ExternalInput").ap()
            for name, v in arrays.items()]
    out = nc.dram_tensor("out", (N, D), F32, kind="ExternalOutput").ap()
    decoder_layer(nc, *args, out)
    got = run_bass_kernel_spmd(nc, [{f"in_{name}": v for name, v in arrays.items()}], core_ids=[0])
    return got.results[0]["out"].reshape(B, S, D)
```
